# Optimizing a Trainium2 kernel written in Bass

```python
import numpy as np
import jax
import jax.numpy as jnp

def _softmax(x, axis=-1):
    return jax.nn.softmax(x, axis=axis)

def _gelu(x):
    return jax.nn.gelu(x, approximate=True)

def _silu(x):
    return jax.nn.silu(x)

def _sigmoid(x):
    return jax.nn.sigmoid(x)

def _layernorm(x, axis=-1, eps=1e-05):
    m = jnp.mean(x, axis=axis, keepdims=True)
    v = jnp.var(x, axis=axis, keepdims=True)
    return (x - m) / jnp.sqrt(v + eps)

def _scatter_add(tgt, idx, src, axis=0):
    return tgt.at[idx].add(src)

def _segment_sum(src, seg, n):
    return jax.ops.segment_sum(src, seg, n)
kernel_name = 'mk_gnn_resnorm_d2_gnn_r32_5f3256'

def setup_inputs(seed: int=0):
    np.random.seed(seed)
    _w = jnp.asarray

    def _rec_inputs():
        import jax
        import jax.numpy as jnp
        _gk = jax.random.key(seed)
        x = -0.0003713 + 1 * jax.random.normal(jax.random.fold_in(_gk, 1), (3125, 128), jnp.float32)
        _s = jax.random.randint(jax.random.fold_in(_gk, 2), (50000,), 0, 3125, jnp.int32)
        _d = jax.random.randint(jax.random.fold_in(_gk, 3), (50000,), 0, 3125, jnp.int32)
        _loop = jnp.arange(3125, dtype=jnp.int32)
        src = jnp.concatenate([_s, _d, _loop])
        dst = jnp.concatenate([_d, _s, _loop])
        _o = jnp.argsort(dst, stable=True)
        src = src[_o]
        dst = dst[_o]
        edge_attr_32 = 0.000312547 + 1.00004 * jax.random.normal(jax.random.fold_in(_gk, 11), (103125, 32), jnp.float32)
        edge_weight = jax.random.uniform(jax.random.fold_in(_gk, 13), (103125,), jnp.float32, 0.0, 1)
        return (x, src, dst, edge_attr_32, edge_weight)
    x, src, dst, edge_attr_32, edge_weight = _rec_inputs()

    def _L0_gnn_setup():
        import jax, jax.numpy as jnp
        import numpy as np
        N = 3125
        E = 15625
        C_IN = 128
        C_OUT = 128
        C_EDGE = 32
        MESSAGE_STEPS = 2

        def _xavier(key, fan_in, fan_out):
            limit = float(np.sqrt(6.0 / (fan_in + fan_out)))
            return jax.random.uniform(key, (fan_in, fan_out), jnp.float32, -limit, limit)
        key = jax.random.key(seed)
        k = jax.random.split(key, 6)
        x = jax.random.normal(k[0], (N, C_IN), jnp.float32)
        edge_index = jax.random.randint(k[1], (2, E), 0, N, jnp.int64)
        edge_attr = jax.random.normal(k[2], (E, C_EDGE), jnp.float32)
        We1 = _xavier(k[3], 2 * C_IN + C_EDGE, C_OUT)
        be1 = jnp.zeros((C_OUT,), jnp.float32)
        We2 = _xavier(k[4], C_OUT, C_OUT)
        be2 = jnp.zeros((C_OUT,), jnp.float32)
        bias = jnp.zeros((C_OUT,), jnp.float32)
        return {'x': x, 'edge_index': edge_index, 'edge_attr': edge_attr, 'We1': We1, 'be1': be1, 'We2': We2, 'be2': be2, 'bias': bias}
    _L0_gnn_all = _L0_gnn_setup()
    _L0_gnn_in = {k: v for k, v in _L0_gnn_all.items() if k in ('We1', 'be1', 'We2', 'be2', 'bias')}
    del _L0_gnn_all

    def _L1_gnn_setup():
        import jax, jax.numpy as jnp
        import numpy as np
        N_NODES = 3125
        N_EDGES = 100000
        D = 128

        def gcn_conv(x, weight, bias, edge_index, edge_weight):
            n = x.shape[0]
            src, dst = (edge_index[0], edge_index[1])
            loop = jnp.arange(n, dtype=src.dtype)
            src = jnp.concatenate([src, loop])
            dst = jnp.concatenate([dst, loop])
            ew = jnp.concatenate([edge_weight, jnp.ones((n,), dtype=edge_weight.dtype)])
            deg = jax.ops.segment_sum(ew, dst, num_segments=n)
            dinv = jnp.where(deg > 0, jax.lax.rsqrt(jnp.where(deg > 0, deg, 1.0)), 0.0)
            norm = dinv[src] * ew * dinv[dst]
            h = x @ weight.T
            msg = h[src] * norm[:, None]
            out = jax.ops.segment_sum(msg, dst, num_segments=n)
            return out + bias
        key = jax.random.key(seed)
        k1, k2, k3, k4, k5 = jax.random.split(key, 5)
        x = jax.random.normal(k1, (N_NODES, D), dtype=jnp.float32)
        weight = jax.random.normal(k2, (D, D), dtype=jnp.float32) * (1.0 / np.sqrt(D))
        bias = jax.random.normal(k3, (D,), dtype=jnp.float32) * 0.01
        edge_weight = jax.random.uniform(k4, (N_EDGES,), dtype=jnp.float32)
        edge_index = jax.random.randint(k5, (2, N_EDGES), 0, N_NODES, dtype=jnp.int64 if jax.config.jax_enable_x64 else jnp.int32)
        return {'x': x, 'weight': weight, 'bias': bias, 'edge_weight': edge_weight, 'edge_index': edge_index}
    _L1_gnn_all = _L1_gnn_setup()
    _L1_gnn_in = {k: v for k, v in _L1_gnn_all.items() if k in ('weight', 'bias')}
    del _L1_gnn_all
    return {'x': x, 'src': src, 'dst': dst, 'edge_attr_32': edge_attr_32, 'edge_weight': edge_weight, 'L0_gnn_We1': _L0_gnn_in['We1'], 'L0_gnn_be1': _L0_gnn_in['be1'], 'L0_gnn_We2': _L0_gnn_in['We2'], 'L0_gnn_be2': _L0_gnn_in['be2'], 'L0_gnn_bias': _L0_gnn_in['bias'], 'L1_gnn_weight': _L1_gnn_in['weight'], 'L1_gnn_bias': _L1_gnn_in['bias']}

def reference(x, src, dst, edge_attr_32, edge_weight, L0_gnn_We1, L0_gnn_be1, L0_gnn_We2, L0_gnn_be2, L0_gnn_bias, L1_gnn_weight, L1_gnn_bias):
    import jax
    import jax.numpy as jnp

    def _L0_gnn_ref(x, edge_index, edge_attr, We1, be1, We2, be2, bias):
        import jax, jax.numpy as jnp
        import numpy as np
        N = 3125
        E = 15625
        C_IN = 128
        C_OUT = 128
        C_EDGE = 32
        MESSAGE_STEPS = 2

        def _xavier(key, fan_in, fan_out):
            limit = float(np.sqrt(6.0 / (fan_in + fan_out)))
            return jax.random.uniform(key, (fan_in, fan_out), jnp.float32, -limit, limit)
        ei = edge_index[0]
        ej = edge_index[1]
        h = x
        for _ in range(MESSAGE_STEPS):
            h_i = h[ei]
            h_j = h[ej]
            edge_input = jnp.concatenate([h_i, h_j, edge_attr], axis=-1)
            m_ij = jax.nn.relu(edge_input @ We1 + be1) @ We2 + be2
            m = jax.ops.segment_sum(m_ij, ej, num_segments=N)
            h = h + m
        return h + bias

    def _L1_gnn_ref(x, weight, bias, edge_weight, edge_index):
        import jax, jax.numpy as jnp
        import numpy as np
        N_NODES = 3125
        N_EDGES = 100000
        D = 128

        def gcn_conv(x, weight, bias, edge_index, edge_weight):
            n = x.shape[0]
            src, dst = (edge_index[0], edge_index[1])
            loop = jnp.arange(n, dtype=src.dtype)
            src = jnp.concatenate([src, loop])
            dst = jnp.concatenate([dst, loop])
            ew = jnp.concatenate([edge_weight, jnp.ones((n,), dtype=edge_weight.dtype)])
            deg = jax.ops.segment_sum(ew, dst, num_segments=n)
            dinv = jnp.where(deg > 0, jax.lax.rsqrt(jnp.where(deg > 0, deg, 1.0)), 0.0)
            norm = dinv[src] * ew * dinv[dst]
            h = x @ weight.T
            msg = h[src] * norm[:, None]
            out = jax.ops.segment_sum(msg, dst, num_segments=n)
            return out + bias
        h = gcn_conv(x, weight, bias, edge_index, edge_weight)
        h = jax.nn.relu(h)
        h = h + x
        return h
    edge_index = jnp.stack([src, dst])
    x = _layernorm(x + _L0_gnn_ref(x, edge_index, edge_attr_32, L0_gnn_We1, L0_gnn_be1, L0_gnn_We2, L0_gnn_be2, L0_gnn_bias), axis=-1)
    x = _layernorm(x + _L1_gnn_ref(x, L1_gnn_weight, L1_gnn_bias, edge_weight, edge_index), axis=-1)
    return x

_drawn_inputs = setup_inputs


def setup_inputs(seed=0):
    import zlib

    import numpy as np

    out = dict(_drawn_inputs(seed))
    spreads = {'L0_gnn_be1': (0.0, 0.1), 'L0_gnn_be2': (0.0, 0.1), 'L0_gnn_bias': (0.0, 2.0)}
    factors = {'edge_weight': 21.334, 'L1_gnn_bias': 8.0}
    for name, (base, spread) in spreads.items():
        noise = np.random.default_rng([zlib.crc32(name.encode()), seed]).standard_normal(out[name].shape)
        drawn = base * np.exp(spread * noise) if base else spread * noise
        out[name] = jnp.asarray(drawn.astype(out[name].dtype))
    for name, factor in factors.items():
        out[name] = (out[name] * factor).astype(out[name].dtype)
    return out
```

```python
import concourse.bass as bass
from concourse import mybir
from contextlib import ExitStack

P = 128
NODES = 3125
EDGES = 103125
CE = 32
TILES = 26
NPAD = TILES * P
CH = 8
HALF = CH // 2
GE = CH * P
NG = -(-EDGES // GE)
PAIRS = (NG - 1) // 2
W = 96
NWIN = -(-NODES // W)
OFF = 8191
BLK = 416
NBLK = NPAD // BLK
EPS = 1e-5
QUADS = [(q, min(4, TILES - q)) for q in range(0, TILES, 4)]
FULL = NODES // P
REST = NODES - FULL * P


def build(nc, x_rows, xT, src_g, dst_row, dst_em, w_em, eaT, We1, be1, We2, be2, bias0, W1T, bias1,
          out, p_dram, q_dram, z_dram, base_dram, span_dram):
    f32, i32 = mybir.dt.float32, mybir.dt.int32
    ALU, ACT, AX = mybir.AluOpType, mybir.ActivationFunctionType, mybir.AxisListType
    ctx = ExitStack()
    with ctx:
        def sb(name, shape, dt=f32):
            return ctx.enter_context(nc.sbuf_tensor(name, shape, dt))

        def sem(name):
            return ctx.enter_context(nc.semaphore(name))

        wpq = sb("wpq", [P, 2, P])
        we2 = sb("we2", [P, P])
        w1t = sb("w1t", [P, P])
        be1_bc = sb("be1_bc", [P, P])
        bias1_bc = sb("bias1_bc", [P, P])
        be2_row = sb("be2_row", [1, P])
        bias0_col = sb("bias0_col", [P, 1])
        ident = sb("ident", [P, P])
        ones = sb("ones", [P, 1])
        eps = sb("eps", [P, 1])
        iota_row = sb("iota_row", [P, W])
        iota_col = sb("iota_col", [P, 1])
        iota_win = sb("iota_win", [P, W])
        hT = sb("hT", [P, NPAD])
        xTs = sb("xTs", [P, NPAD])
        aggT = sb("aggT", [P, NPAD])
        cw = sb("cw", [1, 2, NPAD])
        node_a = sb("node_a", [P, TILES, P])
        node_b = sb("node_b", [P, TILES, P])
        x1 = sb("x1", [P, TILES, P])
        deg = sb("deg", [P, TILES])
        dmask = sb("dmask", [P, TILES])
        dtmp = sb("dtmp", [P, TILES])
        dinv = sb("dinv", [P, TILES])
        stats = sb("stats", [P, TILES, 6])
        mv = sb("mv", [P, TILES, 2])
        std = sb("std", [P, TILES])
        rstd = sb("rstd", [P, TILES])
        dsts = sb("dsts", [P, NG * CH], i32)
        ws = sb("ws", [P, NG * CH])
        drel = sb("drel", [P, NG * CH])
        dgrp = sb("dgrp", [NG, GE], i32)
        dreal = sb("dreal", [NG, GE])
        bmin = sb("bmin", [NG, 1])
        bmax = sb("bmax", [NG, 1])
        span = sb("span", [NG, 1])
        bint = sb("bint", [NG, 1], i32)
        base_row = sb("base_row", [1, NG], i32)
        base_bc = sb("base_bc", [P, NG], i32)
        base_p = sb("base_p", [P, NG])
        span_row = sb("span_row", [1, NG])
        span_max = sb("span_max", [1, 1])
        flag = sb("flag", [1, 1], i32)
        idx = [sb(f"idx{s}", [P, CH], i32) for s in range(2)]
        dbc = [sb(f"dbc{s}", [W, GE], i32) for s in range(2)]
        lhs = [sb(f"lhs{s}", [P, GE]) for s in range(2)]
        rhs = [sb(f"rhs{s}", [P, P]) for s in range(2)]
        gat = [sb(f"gat{s}", [P, CH, P]) for s in range(2)]
        msg = [sb(f"msg{s}", [P, CH, P]) for s in range(2)]
        hot = [sb(f"hot{s}", [P, CH, 2, W]) for s in range(2)]
        idxd = sb("idxd", [P, CH], i32)
        gatq = sb("gatq", [P, CH, P])

        ps = ctx.enter_context(nc.psum_tensor("ps", [P, 8, 512], f32))

        def ps_pre(s, h):
            return ps[:, 2 * s + h, :]

        def ps_agg(s):
            return ps[:, 4 + s, 0:W]

        def ps_cw(s):
            return ps[0:1, 6 + s, 0:2 * W]

        const_in = sem("const_in")
        meta_in = sem("meta_in")
        grp_in = sem("grp_in")
        x_in = sem("x_in")
        base_out = sem("base_out")
        base_in = sem("base_in")
        pool_const = sem("pool_const")
        dve_const = sem("dve_const")
        bounds = sem("bounds")
        flag_ready = sem("flag_ready")
        rel_ready = sem("rel_ready")
        rhs_const = [sem(f"rhs_const{s}") for s in range(2)]
        pq_mm = sem("pq_mm")
        p_copied = sem("p_copied")
        q_copied = sem("q_copied")
        p_out = sem("p_out")
        q_out = sem("q_out")
        m_mm = sem("m_mm")
        m_added = sem("m_added")
        agg_clear = sem("agg_clear")
        idx_in = [sem(f"idx_in{s}") for s in range(2)]
        dbc_in = [sem(f"dbc_in{s}") for s in range(2)]
        ea_in = [sem(f"ea_in{s}") for s in range(2)]
        qw_in = [sem(f"qw_in{s}") for s in range(2)]
        rows_in = [[sem(f"rows_in{s}{h}") for h in range(2)] for s in range(2)]
        passed = sem("passed")
        oht_made = sem("oht_made")
        hot_made = sem("hot_made")
        hotw_made = sem("hotw_made")
        pre_mm = sem("pre_mm")
        pre_added = sem("pre_added")
        relu_done = sem("relu_done")
        scat_mm = sem("scat_mm")
        agg_added = sem("agg_added")
        g_idx = sem("g_idx")
        g_ea = sem("g_ea")
        g_qw = sem("g_qw")
        g_idxd = sem("g_idxd")
        g_rows = sem("g_rows")
        g_rowsq = sem("g_rowsq")
        g_lhs = sem("g_lhs")
        g_pre = sem("g_pre")
        g_add = sem("g_add")
        g_relu = sem("g_relu")
        g_win = sem("g_win")
        g_hot = sem("g_hot")
        g_scat = sem("g_scat")
        g_agg = sem("g_agg")
        g_group = sem("g_group")
        u_ready = sem("u_ready")
        deg_mm = sem("deg_mm")
        dchain = sem("dchain")
        u_tr = sem("u_tr")
        u_copied = sem("u_copied")
        ln_stats = sem("ln_stats")
        ln_var = sem("ln_var")
        ln_std = sem("ln_std")
        ln_rstd = sem("ln_rstd")
        x1_made = sem("x1_made")
        z_made = sem("z_made")
        z_out = sem("z_out")
        z_tr = sem("z_tr")
        z_copied = sem("z_copied")
        x2_made = sem("x2_made")
        y_mm = sem("y_mm")
        y_scaled = sem("y_scaled")
        y_made = sem("y_made")
        out_made = sem("out_made")
        out_out = sem("out_out")

        block = ctx.enter_context(nc.Block())

        def nth(p, g):
            return p * NG + g

        def slot_dma(p, g, s):
            return p * (PAIRS + (1 if s == 0 else 0)) + (g - s) // 2 + 1

        def groups(eng, step):
            step(0, 0, 1, True)
            step(1, 1, 1, True)
            with eng.Fori(1, PAIRS) as j:
                step(2 * j, 0, j + 1, False)
                step(2 * j + 1, 1, j + 1, False)
            step(NG - 1, 0, PAIRS + 1, False)

        def used(p, s, k):
            return p * (PAIRS + (1 if s == 0 else 0)) + k

        @block.sync
        def _(sp):
            sp.dma_start(dgrp[:, :], dst_row.rearrange("(g e) -> g e", e=GE)).then_inc(grp_in, 16)
            sp.dma_start(hT[:, 0:NODES], xT).then_inc(x_in, 16)
            sp.dma_start(wpq[:, :, :], We1[0:2 * P, :].rearrange("(a f) n -> f a n", a=2)).then_inc(const_in, 16)
            sp.dma_start(we2[:, :], We2).then_inc(const_in, 16)
            sp.dma_start(w1t[:, :], W1T).then_inc(const_in, 16)
            sp.dma_start(be1_bc[:, :], be1.rearrange("(a n) -> a n", a=1).to_broadcast([P, P])).then_inc(const_in, 16)
            sp.dma_start(bias1_bc[:, :], bias1.rearrange("(a n) -> a n", a=1).to_broadcast([P, P])).then_inc(const_in, 16)
            sp.dma_start(be2_row[:, :], be2.rearrange("(a n) -> a n", a=1)).then_inc(const_in, 16)
            sp.dma_start(bias0_col[:, :], bias0.rearrange("(n a) -> n a", a=1)).then_inc(const_in, 16)
            for s in range(2):
                sp.dma_start(rhs[s][W:P, :], We1[2 * P:2 * P + CE, :]).then_inc(rhs_const[s], 16)
            sp.dma_start(xTs[:, 0:NODES], xT).then_inc(x_in, 16)
            sp.dma_start(dsts[:, :], dst_em).then_inc(meta_in, 16)
            sp.dma_start(ws[:, :], w_em).then_inc(meta_in, 16)
            sp.wait_ge(bounds, 5)
            sp.dma_start(base_dram.rearrange("(n a) -> n a", a=1), bint[:, :]).then_inc(base_out, 16)
            sp.dma_start(span_dram.rearrange("(n a) -> n a", a=1), span[:, :]).then_inc(base_out, 16)
            sp.wait_ge(base_out, 32)
            brow = base_dram.rearrange("(a n) -> a n", a=1)
            sp.dma_start(base_row[:, :], brow).then_inc(base_in, 16)
            sp.dma_start(base_bc[:, :], brow.to_broadcast([P, NG])).then_inc(base_in, 16)
            sp.dma_start(span_row[:, :], span_dram.rearrange("(a n) -> a n", a=1)).then_inc(base_in, 16)
            sp.wait_ge(base_in, 48)
            sp.wait_ge(flag_ready, 1)
            fast = sp.value_load(flag[0:1, 0:1], min_val=0, max_val=1)

            for p in range(3):
                if p < 2:
                    for q, (t0, n) in enumerate(QUADS):
                        pairs = 13 * p + (t0 + n) // 2
                        sp.wait_ge(p_copied, pairs)
                        sp.dma_start(p_dram.rearrange("(t p) f -> p t f", p=P)[:, t0:t0 + n, :],
                                     node_a[:, t0:t0 + n, :]).then_inc(p_out, 16)
                        sp.wait_ge(q_copied, pairs)
                        sp.dma_start(q_dram.rearrange("(t p) f -> p t f", p=P)[:, t0:t0 + n, :],
                                     node_b[:, t0:t0 + n, :]).then_inc(q_out, 16)
                    sp.wait_ge(q_out, 16 * len(QUADS) * (p + 1))
                else:
                    for q, (t0, n) in enumerate(QUADS):
                        sp.wait_ge(z_made, t0 + n)
                        sp.dma_start(z_dram.rearrange("(t p) f -> p t f", p=P)[:, t0:t0 + n, :],
                                     node_b[:, t0:t0 + n, :]).then_inc(z_out, 16)
                with sp.If(fast == 1):
                    def load(g, s, k, first):
                        old = p > 0 or not first
                        if old:
                            sp.wait_ge(rows_in[s][1], 16 * HALF * (used(p, s, k) - 1))
                        sp.dma_start(idx[s][:, :], src_g[bass.ds(g, 1), :, :].rearrange("a p k -> (a p) k")
                                     ).then_inc(idx_in[s], 16)
                        if p == 2:
                            return
                        if old:
                            sp.wait_ge(oht_made, nth(p, g) - 1)
                        row = dst_row[bass.ds(g * GE, GE)].rearrange("(a n) -> a n", a=1)
                        sp.dma_start(dbc[s][:, :], row.to_broadcast([W, GE])).then_inc(dbc_in[s], 16)
                        if old:
                            sp.wait_ge(pre_mm, 2 * (nth(p, g) - 1))
                        sp.dma_start(lhs[s][W:P, :], eaT[:, bass.ds(g * GE, GE)]).then_inc(ea_in[s], 16)
                        sp.sem_inc(passed, 1)
                        b = sp.value_load(base_row[0:1, bass.ds(g, 1)], min_val=0, max_val=NODES - 1)
                        sp.dma_start(rhs[s][0:W, :], q_dram[bass.ds(b, W), :]).then_inc(qw_in[s], 16)
                    groups(sp, load)
                with sp.Else():
                    with sp.Fori(0, NG) as g:
                        sp.wait_ge(g_group, nth(p, g) + 1)
                        sp.dma_start(idx[0][:, :], src_g[bass.ds(g, 1), :, :].rearrange("a p k -> (a p) k")
                                     ).then_inc(g_idx, 16)
                        if p < 2:
                            sp.dma_start(lhs[0][W:P, :], eaT[:, bass.ds(g * GE, GE)]).then_inc(g_ea, 16)
                            sp.dma_start(rhs[0][0:W, :], q_dram[0:W, :]).then_inc(g_qw, 16)
            for q, (t0, n) in enumerate(QUADS):
                sp.wait_ge(out_made, t0 + n)
                full = min(n, FULL - t0)
                sp.dma_start(out[t0 * P:(t0 + full) * P, :].rearrange("(t p) f -> p t f", p=P) if full > 0 else
                             out[FULL * P:NODES, :],
                             node_b[:, t0:t0 + full, :] if full > 0 else node_b[0:REST, FULL, :]).then_inc(out_out, 16)
            sp.wait_ge(out_out, 16 * len(QUADS))
            sp.wait_ge(p_out, 32 * len(QUADS))
            sp.wait_ge(q_out, 32 * len(QUADS))
            sp.wait_ge(z_out, 16 * len(QUADS))

        @block.gpsimd
        def _(pool):
            pool.iota(iota_row[:, :], pattern=[[1, W]], base=0, channel_multiplier=0,
                      allow_small_or_imprecise_dtypes=True).then_inc(pool_const, 1)
            pool.iota(iota_col[:, :], pattern=[[0, 1]], base=0, channel_multiplier=1,
                      allow_small_or_imprecise_dtypes=True).then_inc(pool_const, 1)
            pool.memset(ident[:, :], 0.0).then_inc(pool_const, 1)
            pool.wait_ge(pool_const, 3)
            pool.affine_select(out=ident[:, :], in_=ident[:, :], compare_op=ALU.not_equal, fill=1.0,
                               base=0, pattern=[[-1, P]], channel_multiplier=1).then_inc(pool_const, 1)
            pool.wait_ge(flag_ready, 1)
            fast = pool.value_load(flag[0:1, 0:1], min_val=0, max_val=1)

            def rows(out_, table, index):
                return pool.indirect_dma_start(out=out_, out_offset=None, in_=table,
                                               in_offset=bass.IndirectOffsetOnAxis(ap=index, axis=0))
            for p in range(3):
                table = p_dram if p < 2 else z_dram
                if p < 2:
                    pool.wait_ge(p_out, 16 * len(QUADS) * (p + 1))
                else:
                    pool.wait_ge(z_out, 16 * len(QUADS))
                with pool.If(fast == 1):
                    def gather(g, s, k, first):
                        pool.wait_ge(idx_in[s], 16 * used(p, s, k))
                        for h in range(2):
                            if p == 2:
                                pool.wait_ge(scat_mm, nth(p, g) - 1)
                            elif p > 0 or not first:
                                pool.wait_ge(pre_added, 2 * (nth(p, g) - 2) + h + 1)
                            pool.sem_inc(passed, 1)
                            for c in range(h * HALF, (h + 1) * HALF):
                                rows(gat[s][:, c, :], table, idx[s][:, c:c + 1]).then_inc(rows_in[s][h], 16)
                    groups(pool, gather)
                with pool.Else():
                    with pool.Fori(0, NG) as g:
                        pool.wait_ge(g_idx, 16 * (nth(p, g) + 1))
                        pool.sem_inc(passed, 1)
                        for c in range(CH):
                            rows(gat[0][:, c, :], table, idx[0][:, c:c + 1]).then_inc(g_rows, 16)
                        if p < 2:
                            pool.wait_ge(g_idxd, nth(p, g) + 1)
                            pool.sem_inc(passed, 1)
                            for c in range(CH):
                                rows(gatq[:, c, :], q_dram, idxd[:, c:c + 1]).then_inc(g_rowsq, 16)

        @block.tensor
        def _(pe):
            pe.wait_ge(flag_ready, 1)
            fast = pe.value_load(flag[0:1, 0:1], min_val=0, max_val=1)
            pe.wait_ge(const_in, 16 * 7)
            pe.wait_ge(pool_const, 4)
            pe.wait_ge(dve_const, 5)
            for s in range(2):
                pe.wait_ge(rhs_const[s], 16)
            pe.wait_ge(x_in, 32)

            def pre_products(s, h):
                for c in range(h * HALF, (h + 1) * HALF):
                    last = nc.tensor.matmul(ps_pre(s, h)[:, (c % HALF) * P:(c % HALF + 1) * P],
                                            lhs[s][:, c * P:(c + 1) * P], rhs[s][:, :], start=True, stop=True)
                return last

            def scatter_products(p, s):
                if p == 0:
                    for c in range(CH):
                        nc.tensor.matmul(ps_cw(s), ones[:, 0:1], hot[s][:, c, :, :].rearrange("p a w -> p (a w)"),
                                         start=(c == 0), stop=(c == CH - 1))
                for c in range(CH):
                    last = nc.tensor.matmul(ps_agg(s), (msg if p < 2 else gat)[s][:, c, :],
                                            hot[s][:, c, (0 if p < 2 else 1), :], start=(c == 0), stop=(c == CH - 1))
                return last

            for p in range(3):
                if p < 2:
                    for t in range(TILES):
                        pair = 13 * p + t // 2
                        if p:
                            pe.wait_ge(m_added, NBLK * (p - 1) + -(-(t + 1) * P // BLK))
                        if t % 2 == 0 and t >= 4:
                            pe.wait_ge(p_copied, pair - 1)
                            pe.wait_ge(q_copied, pair - 1)
                        for a in range(2):
                            mm = nc.tensor.matmul(ps[:, 2 * (t // 2 % 2) + a, (t % 2) * P:(t % 2 + 1) * P],
                                                  hT[:, t * P:(t + 1) * P], wpq[:, a, :], start=True, stop=True)
                        if t % 2:
                            mm.then_inc(pq_mm, 1)
                    pe.wait_ge(p_copied, 13 * (p + 1))
                    pe.wait_ge(q_copied, 13 * (p + 1))
                with pe.If(fast == 1):
                    def products(g, s, k, first):
                        n = nth(p, g)
                        if p < 2:
                            pe.wait_ge(oht_made, n + 1)
                            pe.wait_ge(ea_in[s], 16 * used(p, s, k))
                            pe.wait_ge(qw_in[s], 16 * used(p, s, k))
                            for h in range(2):
                                if p > 0 or not first:
                                    pe.wait_ge(pre_added, 2 * (n - 2) + h + 1)
                                pre_products(s, h).then_inc(pre_mm, 1)
                            pe.wait_ge(relu_done, 2 * n + 2)
                        else:
                            for h in range(2):
                                pe.wait_ge(rows_in[s][h], 16 * HALF * used(p, s, k))
                        if p != 1:
                            pe.wait_ge(hotw_made, (0 if p == 0 else NG) + g + 1)
                        else:
                            pe.wait_ge(hot_made, n + 1)
                        if p > 0 or not first:
                            pe.wait_ge(agg_added, n - 1)
                        scatter_products(p, s).then_inc(scat_mm, 1)
                    groups(pe, products)
                with pe.Else():
                    with pe.Fori(0, NG) as g:
                        n = nth(p, g)
                        if p < 2:
                            pe.wait_ge(g_lhs, n + 1)
                            pe.wait_ge(g_ea, 16 * (n + 1))
                            pe.wait_ge(g_qw, 16 * (n + 1))
                            for h in range(2):
                                last = pre_products(0, h)
                            last.then_inc(g_pre, 1)
                            pe.wait_ge(g_relu, n + 1)
                        else:
                            pe.wait_ge(g_rows, 16 * CH * (n + 1))
                        pe.sem_inc(passed, 1)
                        with pe.Fori(0, NWIN) as w:
                            pe.wait_ge(g_hot, n * NWIN + w + 1)
                            scatter_products(p, 0).then_inc(g_scat, 1)
                if p < 2:
                    pe.wait_ge(agg_clear, 2 * p + 1)
                    for b in range(NBLK):
                        if b >= 4:
                            pe.wait_ge(m_added, NBLK * p + b - 3)
                        cols = slice(b * BLK, (b + 1) * BLK)
                        nc.tensor.matmul(ps[:, 4 + b % 4, 0:BLK], we2[:, :], aggT[:, cols], start=True, stop=False)
                        nc.tensor.matmul(ps[:, 4 + b % 4, 0:BLK], be2_row[:, :], cw[0:1, 0, cols],
                                         start=False, stop=True).then_inc(m_mm, 1)
                if p == 1:
                    pe.wait_ge(m_added, 2 * NBLK)
                    for t in range(TILES):
                        mm = nc.tensor.matmul(ps[:, 7, t:t + 1], cw[0:1, 1, t * P:(t + 1) * P], ones[0:1, 0:1],
                                              start=True, stop=True)
                    mm.then_inc(deg_mm, 1)
                    pe.wait_ge(u_ready, 1)
                    for q, (t0, n) in enumerate(QUADS):
                        if q >= 4:
                            pe.wait_ge(u_copied, q - 3)
                        for t in range(t0, t0 + n):
                            tr = nc.tensor.transpose(ps[:, q % 4, (t - t0) * P:(t - t0 + 1) * P],
                                                     hT[:, t * P:(t + 1) * P], ident[:, :])
                        tr.then_inc(u_tr, 1)
                    pe.wait_ge(u_copied, len(QUADS))
                    for q, (t0, n) in enumerate(QUADS):
                        pe.wait_ge(z_made, t0 + n)
                        if q >= 4:
                            pe.wait_ge(z_copied, q - 3)
                        for t in range(t0, t0 + n):
                            tr = nc.tensor.transpose(ps[:, q % 4, (t - t0) * P:(t - t0 + 1) * P],
                                                     node_b[:, t, :], ident[:, :])
                        tr.then_inc(z_tr, 1)
                    pe.wait_ge(z_copied, len(QUADS))
            pe.wait_ge(agg_clear, 5)
            for q, (t0, n) in enumerate(QUADS):
                if q >= 4:
                    pe.wait_ge(y_scaled, t0 - 12)
                for t in range(t0, t0 + n):
                    mm = nc.tensor.matmul(ps[:, q % 4, (t - t0) * P:(t - t0 + 1) * P],
                                          aggT[:, t * P:(t + 1) * P], w1t[:, :], start=True, stop=True)
                mm.then_inc(y_mm, 1)

        @block.scalar
        def _(act):
            act.wait_ge(flag_ready, 1)
            fast = act.value_load(flag[0:1, 0:1], min_val=0, max_val=1)
            for p in range(3):
                if p < 2:
                    if p:
                        act.wait_ge(p_out, 16 * len(QUADS))
                    for j in range(TILES // 2):
                        act.wait_ge(pq_mm, 13 * p + j + 1)
                        nc.scalar.copy(node_a[:, 2 * j:2 * j + 2, :],
                                       ps[:, 2 * (j % 2), 0:2 * P].rearrange("p (t f) -> p t f", t=2)
                                       ).then_inc(p_copied, 1)
                    with act.If(fast == 1):
                        def relu(g, s, k, first):
                            for h in range(2):
                                act.wait_ge(pre_added, 2 * nth(p, g) + h + 1)
                                m = msg[s][:, h * HALF:(h + 1) * HALF, :]
                                nc.scalar.activation(m, m, ACT.Relu).then_inc(relu_done, 1)
                        groups(act, relu)
                    with act.Else():
                        with act.Fori(0, NG) as g:
                            act.wait_ge(g_add, 2 * nth(p, g) + 2)
                            nc.scalar.activation(msg[0][:, :, :], msg[0][:, :, :], ACT.Relu).then_inc(g_relu, 1)
                if p == 1:
                    act.wait_ge(p_out, 2 * 16 * len(QUADS))
                    for q, (t0, n) in enumerate(QUADS):
                        act.wait_ge(u_tr, q + 1)
                        nc.scalar.copy(node_a[:, t0:t0 + n, :],
                                       ps[:, q % 4, 0:n * P].rearrange("p (t f) -> p t f", f=P)).then_inc(u_copied, 1)
                    act.wait_ge(dchain, 3)
                    nc.scalar.activation(dtmp[:, :], dtmp[:, :], ACT.Sqrt).then_inc(ln_std, 1)
                    act.wait_ge(ln_var, TILES)
                    nc.scalar.activation(std[:, :], mv[:, :, 1], ACT.Sqrt, bias=eps[:, 0:1]).then_inc(ln_std, 1)
                    act.wait_ge(q_out, 2 * 16 * len(QUADS))
                    act.wait_ge(dchain, 5)
                    for t in range(TILES):
                        act.wait_ge(x1_made, t + 1)
                        nc.scalar.mul(node_b[:, t, :], x1[:, t, :], dinv[:, t:t + 1]).then_inc(z_made, 1)
                    for q, (t0, n) in enumerate(QUADS):
                        act.wait_ge(z_tr, q + 1)
                        nc.scalar.copy(aggT[:, t0 * P:(t0 + n) * P], ps[:, q % 4, 0:n * P]).then_inc(z_copied, 1)
            act.wait_ge(ln_var, 2 * TILES)
            nc.scalar.activation(std[:, :], mv[:, :, 1], ACT.Sqrt, bias=eps[:, 0:1]).then_inc(ln_std, 1)

        @block.vector
        def _(dve):
            V = nc.vector
            V.memset(ones[:, :], 1.0).then_inc(dve_const, 1)
            V.memset(eps[:, :], EPS).then_inc(dve_const, 1)
            V.memset(aggT[:, :], 0.0).then_inc(dve_const, 1)
            V.memset(cw[:, :, :], 0.0).then_inc(dve_const, 1)
            V.memset(hT[:, NODES:NPAD], 0.0).then_inc(dve_const, 1)
            V.memset(xTs[:, NODES:NPAD], 0.0).then_inc(dve_const, 1)
            dve.wait_ge(grp_in, 16)
            V.tensor_reduce(bmin[:, :], dgrp[:, :], AX.X, ALU.min).then_inc(bounds, 1)
            V.scalar_tensor_tensor(dreal[:, :], dgrp[:, :], float(NODES), dgrp[:, :], ALU.is_lt, ALU.mult
                                   ).then_inc(bounds, 1)
            dve.wait_ge(bounds, 2)
            V.tensor_reduce(bmax[:, :], dreal[:, :], AX.X, ALU.max).then_inc(bounds, 1)
            V.tensor_copy(bint[:, :], bmin[:, :]).then_inc(bounds, 1)
            dve.wait_ge(bounds, 4)
            V.tensor_tensor(span[:, :], bmax[:, :], bmin[:, :], ALU.subtract).then_inc(bounds, 1)
            dve.wait_ge(base_in, 48)
            V.tensor_reduce(span_max[:, :], span_row[:, :], AX.X, ALU.max).then_inc(bounds, 1)
            dve.wait_ge(bounds, 6)
            V.tensor_single_scalar(flag[:, :], span_max[:, :], float(W), ALU.is_lt).then_inc(flag_ready, 1)
            dve.wait_ge(pool_const, 4)
            V.tensor_scalar(base_p[:, :], base_bc[:, :], iota_col[:, 0:1], None, ALU.add).then_inc(rel_ready, 1)
            dve.wait_ge(meta_in, 32)
            V.tensor_tensor(drel[:, :].rearrange("p (g c) -> p g c", c=CH),
                            dsts[:, :].rearrange("p (g c) -> p g c", c=CH),
                            base_bc[:, :].unsqueeze(2).to_broadcast([P, NG, CH]), ALU.subtract).then_inc(rel_ready, 1)
            dve.wait_ge(flag_ready, 1)
            fast = dve.value_load(flag[0:1, 0:1], min_val=0, max_val=1)
            dve.wait_ge(rel_ready, 2)
            dve.wait_ge(dve_const, 6)
            dve.wait_ge(const_in, 16 * 7)

            def one_hot(s, ids, window):
                return V.tensor_tensor(hot[s][:, :, 0, :], window[:, :].unsqueeze(1).to_broadcast([P, CH, W]),
                                       ids.unsqueeze(2).to_broadcast([P, CH, W]), ALU.is_equal)

            def weigh(s, g):
                return V.tensor_tensor(hot[s][:, :, 1, :], hot[s][:, :, 0, :],
                                       ws[:, bass.ds(g * CH, CH)].unsqueeze(2).to_broadcast([P, CH, W]), ALU.mult)

            for p in range(3):
                if p < 2:
                    if p:
                        dve.wait_ge(q_out, 16 * len(QUADS))
                    for j in range(TILES // 2):
                        dve.wait_ge(pq_mm, 13 * p + j + 1)
                        V.tensor_tensor(node_b[:, 2 * j:2 * j + 2, :],
                                        ps[:, 2 * (j % 2) + 1, 0:2 * P].rearrange("p (t f) -> p t f", t=2),
                                        be1_bc[:, :].unsqueeze(1).to_broadcast([P, 2, P]), ALU.add
                                        ).then_inc(q_copied, 1)
                else:
                    dve.wait_ge(z_copied, len(QUADS))
                with dve.If(fast == 1):
                    def add_window(g, s):
                        n = nth(p, g)
                        dve.sem_inc(passed, 1)
                        b = dve.value_load(base_row[0:1, bass.ds(g, 1)], min_val=0, max_val=NODES - 1)
                        dve.wait_ge(scat_mm, n + 1)
                        if p == 0:
                            c = cw[0:1, :, bass.ds(b, W)]
                            V.tensor_tensor(c, c, ps_cw(s).rearrange("p (a w) -> p a w", a=2), ALU.add)
                        a = aggT[:, bass.ds(b, W)]
                        V.tensor_tensor(a, a, ps_agg(s), ALU.add).then_inc(agg_added, 1)

                    def vector_step(g, s, k, first, before=True):
                        n = nth(p, g)
                        old = p > 0 or not first
                        if p < 2:
                            dve.wait_ge(dbc_in[s], 16 * used(p, s, k))
                            if old:
                                dve.wait_ge(pre_mm, 2 * (n - 1))
                            V.tensor_scalar(lhs[s][0:W, :], dbc[s][:, :], base_p[0:W, bass.ds(g, 1)], None,
                                            ALU.is_equal).then_inc(oht_made, 1)
                        if old:
                            dve.wait_ge(scat_mm, n - 1)
                        one_hot(s, drel[:, bass.ds(g * CH, CH)], iota_row).then_inc(hot_made, 1)
                        if p != 1:
                            dve.wait_ge(hot_made, n + 1)
                            weigh(s, g).then_inc(hotw_made, 1)
                        if p > 0 or before:
                            if before:
                                if p > 0 or not (first and g == 1) or True:
                                    if not (p == 0 and first and g == 1):
                                        dve.wait_ge(agg_added, n - 1)
                                add_window(g - 1, 1 - s)
                        if p < 2:
                            for h in range(2):
                                dve.wait_ge(rows_in[s][h], 16 * HALF * used(p, s, k))
                                dve.wait_ge(pre_mm, 2 * n + h + 1)
                                V.tensor_tensor(msg[s][:, h * HALF:(h + 1) * HALF, :],
                                                ps_pre(s, h).rearrange("p (c f) -> p c f", f=P),
                                                gat[s][:, h * HALF:(h + 1) * HALF, :], ALU.add).then_inc(pre_added, 1)

                    vector_step(0, 0, 1, True, before=False)
                    vector_step(1, 1, 1, True)
                    with dve.Fori(1, PAIRS) as j:
                        vector_step(2 * j, 0, j + 1, False)
                        vector_step(2 * j + 1, 1, j + 1, False)
                    vector_step(NG - 1, 0, PAIRS + 1, False)
                    dve.wait_ge(agg_added, nth(p, NG - 1))
                    add_window(NG - 1, 0)
                    dve.wait_ge(agg_added, nth(p, NG))
                    V.memset(span_max[:, :], 0.0).then_inc(agg_clear, 1)
                with dve.Else():
                    if p == 0:
                        V.memset(lhs[0][0:W, :], 0.0).then_inc(g_group, 1)
                    with dve.Fori(0, NG) as g:
                        n = nth(p, g)
                        dve.wait_ge(g_group, n + 1)
                        if p < 2:
                            V.tensor_single_scalar(idxd[:, :], dsts[:, bass.ds(g * CH, CH)], float(NPAD - 1),
                                                   ALU.min).then_inc(g_idxd, 1)
                            V.memset(iota_win[:, :], 0.0).then_inc(g_lhs, 1)
                            dve.wait_ge(g_rows, 16 * CH * (n + 1))
                            dve.wait_ge(g_pre, n + 1)
                            V.tensor_tensor(msg[0][:, :, :], ps[:, 0:2, :].rearrange("p h (c f) -> p (h c) f", f=P),
                                            gat[0][:, :, :], ALU.add).then_inc(g_add, 1)
                            dve.wait_ge(g_rowsq, 16 * CH * (n + 1))
                            dve.wait_ge(g_add, 2 * n + 1)
                            V.tensor_tensor(msg[0][:, :, :], msg[0][:, :, :], gatq[:, :, :], ALU.add
                                            ).then_inc(g_add, 1)
                            dve.wait_ge(g_add, 2 * n + 2)
                        V.tensor_copy(iota_win[:, :], iota_row[:, :]).then_inc(g_win, 1)
                        with dve.Fori(0, NWIN) as w:
                            m = n * NWIN + w
                            dve.wait_ge(g_win, n * (NWIN + 1) + w + 1)
                            one_hot(0, dsts[:, bass.ds(g * CH, CH)], iota_win).then_inc(hot_made, 1)
                            dve.wait_ge(hot_made, m + 1)
                            weigh(0, g).then_inc(g_hot, 1)
                            V.tensor_scalar_add(iota_win[:, :], iota_win[:, :], float(W)).then_inc(g_win, 1)
                            dve.wait_ge(g_scat, m + 1)
                            if p == 0:
                                V.tensor_tensor(cw[0:1, :, bass.ds(w * W, W)], cw[0:1, :, bass.ds(w * W, W)],
                                                ps_cw(0).rearrange("p (a w) -> p a w", a=2), ALU.add)
                            V.tensor_tensor(aggT[:, bass.ds(w * W, W)], aggT[:, bass.ds(w * W, W)], ps_agg(0),
                                            ALU.add).then_inc(g_agg, 1)
                            dve.wait_ge(g_agg, m + 1)
                        V.memset(span_max[:, :], 0.0).then_inc(g_group, 1)
                    dve.wait_ge(g_group, nth(p, NG) + 1)
                    V.memset(span_max[:, :], 0.0).then_inc(agg_clear, 1)
                if p < 2:
                    for b in range(NBLK):
                        cols = slice(b * BLK, (b + 1) * BLK)
                        dve.wait_ge(m_mm, NBLK * p + b + 1)
                        V.tensor_tensor(hT[:, cols], hT[:, cols], ps[:, 4 + b % 4, 0:BLK], ALU.add).then_inc(m_added, 1)
                    dve.wait_ge(agg_clear, 2 * p + 1)
                    V.memset(aggT[:, :], 0.0).then_inc(agg_clear, 1)
                    dve.wait_ge(agg_clear, 2 * p + 2)
                if p == 1:
                    dve.wait_ge(m_added, 2 * NBLK)
                    V.scalar_tensor_tensor(hT[:, :], hT[:, :], bias0_col[:, 0:1], xTs[:, :], ALU.add, ALU.add
                                           ).then_inc(u_ready, 1)
                    dve.wait_ge(deg_mm, 1)
                    V.tensor_scalar_add(deg[:, :], ps[:, 7, 0:TILES], 1.0).then_inc(dchain, 1)
                    dve.wait_ge(dchain, 1)
                    V.tensor_single_scalar(dmask[:, :], deg[:, :], 0.0, ALU.is_gt).then_inc(dchain, 1)
                    dve.wait_ge(dchain, 2)
                    V.tensor_copy(dtmp[:, :], ones[:, 0:1].to_broadcast([P, TILES])).then_inc(bounds, 1)
                    dve.wait_ge(bounds, 7)
                    V.copy_predicated(dtmp[:, :], dmask[:, :].bitcast(mybir.dt.uint32), deg[:, :]).then_inc(dchain, 1)
                    dve.wait_ge(ln_std, 1)
                    V.reciprocal(dtmp[:, :], dtmp[:, :]).then_inc(dchain, 1)
                    dve.wait_ge(dchain, 4)
                    V.tensor_tensor(dinv[:, :], dtmp[:, :], dmask[:, :], ALU.mult).then_inc(dchain, 1)

                def layer_norm(which, src, made, dst):
                    for t in range(TILES):
                        made(t)
                        V.bn_stats(stats[:, t, :], src[:, t, :]).then_inc(ln_stats, 1)
                    for t in range(TILES):
                        dve.wait_ge(ln_stats, which * TILES + t + 1)
                        V.bn_aggr(mv[:, t, :], stats[:, t, :]).then_inc(ln_var, 1)
                    dve.wait_ge(ln_std, which + 2)
                    V.reciprocal(rstd[:, :], std[:, :]).then_inc(ln_rstd, 1)
                    dve.wait_ge(ln_rstd, which + 1)
                    for t in range(TILES):
                        V.tensor_scalar(dst[:, t, :], src[:, t, :], mv[:, t, 0:1], rstd[:, t:t + 1],
                                        ALU.subtract, ALU.mult).then_inc(x1_made if which == 0 else out_made, 1)

                if p == 1:
                    layer_norm(0, node_a, lambda t: dve.wait_ge(u_copied, t // 4 + 1), x1)
                    dve.wait_ge(x1_made, TILES)
                    dve.wait_ge(z_made, TILES)
                    V.tensor_scalar_mul(x1[:, :, :], x1[:, :, :], 2.0).then_inc(x2_made, 1)
            dve.wait_ge(x2_made, 1)
            for t in range(TILES):
                dve.wait_ge(y_mm, t // 4 + 1)
                V.scalar_tensor_tensor(node_a[:, t, :], ps[:, (t // 4) % 4, (t % 4) * P:(t % 4 + 1) * P],
                                       dinv[:, t:t + 1], bias1_bc[:, :], ALU.mult, ALU.add).then_inc(y_scaled, 1)
                dve.wait_ge(y_scaled, t + 1)
                V.scalar_tensor_tensor(node_a[:, t, :], node_a[:, t, :], 0.0, x1[:, t, :], ALU.max, ALU.add
                                       ).then_inc(y_made, 1)
            dve.wait_ge(z_out, 16 * len(QUADS))
            layer_norm(1, node_a, lambda t: dve.wait_ge(y_made, t + 1), node_b)


def kernel(**inputs):
    import numpy as np
    import concourse.bacc as bacc
    from concourse.bass_utils import run_bass_kernel_spmd

    f32, i32 = mybir.dt.float32, mybir.dt.int32
    pad = NG * GE - EDGES
    src = np.concatenate([np.asarray(inputs["src"]), np.zeros(pad, np.int32)])
    dst = np.concatenate([np.asarray(inputs["dst"]), np.full(pad, OFF, np.int32)])
    ew = np.concatenate([np.asarray(inputs["edge_weight"]), np.zeros(pad, np.float32)])
    ea = np.concatenate([np.asarray(inputs["edge_attr_32"]), np.zeros((pad, CE), np.float32)])
    by_lane = lambda a: np.ascontiguousarray(a.reshape(NG * CH, P).T)
    arrays = {
        "xT": np.ascontiguousarray(np.asarray(inputs["x"]).T),
        "src_g": np.ascontiguousarray(src.reshape(NG, CH, P).transpose(0, 2, 1)),
        "dst_row": dst, "dst_em": by_lane(dst), "w_em": by_lane(ew),
        "eaT": np.ascontiguousarray(ea.T),
        "We1": np.asarray(inputs["L0_gnn_We1"]), "be1": np.asarray(inputs["L0_gnn_be1"]),
        "We2": np.asarray(inputs["L0_gnn_We2"]), "be2": np.asarray(inputs["L0_gnn_be2"]),
        "bias0": np.asarray(inputs["L0_gnn_bias"]),
        "W1T": np.ascontiguousarray(np.asarray(inputs["L1_gnn_weight"]).T),
        "bias1": np.asarray(inputs["L1_gnn_bias"]),
    }
    nc = bacc.Bacc("TRN2", target_bir_lowering=False, num_devices=1)
    args = {n: nc.dram_tensor(n, a.shape, mybir.dt.from_np(a.dtype), kind="ExternalInput").ap()
            for n, a in arrays.items()}
    out = nc.dram_tensor("out", (NODES, P), f32, kind="ExternalOutput").ap()
    scratch = {n: nc.dram_tensor(n, (NPAD, P), f32, kind="Internal").ap() for n in ("p_dram", "q_dram", "z_dram")}
    build(nc, None, out=out, base_dram=nc.dram_tensor("base_dram", (NG,), i32, kind="Internal").ap(),
          span_dram=nc.dram_tensor("span_dram", (NG,), f32, kind="Internal").ap(), **scratch, **args)
    r = run_bass_kernel_spmd(nc, [arrays], core_ids=[0])
    return r.results[0]["out"]
```

```python
import concourse.bass as bass
from concourse import mybir
from contextlib import ExitStack

P = 128
NODES = 3125
EDGES = 103125
CE = 32
TILES = 26
NPAD = TILES * P
CH = 8
HALF = CH // 2
GE = CH * P
NG = -(-EDGES // GE)
PAIRS = (NG - 1) // 2
W = 64
CW = 8
HI = -(-NODES // P)
KEYS = HI * CW
NWIN = -(-NODES // W)
OFF = 8191
BLK = 416
NBLK = NPAD // BLK
EPS = 1e-5
TURN = "EP" * 10
TURNS = NG // len(TURN)
E_TURN, P_TURN = TURN.count("E"), TURN.count("P")
E_LAST = E_TURN * TURNS
P_LAST = P_TURN * TURNS
E_LAG, P_LAG = 4, 2
QUADS = [(q, min(4, TILES - q)) for q in range(0, TILES, 4)]
FULL = NODES // P
REST = NODES - FULL * P


def build(nc, xT, src_g, src_em, dst_row, dst_em, w_em, eaT, We1, be1, We2, be2, bias0, W1T, bias1,
          out, p_dram, q_dram, z_dram, base_dram, span_dram, cbase_dram):
    f32, bf16, i32 = mybir.dt.float32, mybir.dt.bfloat16, mybir.dt.int32
    ALU, ACT, AX = mybir.AluOpType, mybir.ActivationFunctionType, mybir.AxisListType
    ctx = ExitStack()
    with ctx:
        def sb(name, shape, dt=f32):
            return ctx.enter_context(nc.sbuf_tensor(name, shape, dt))

        def sem(name):
            return ctx.enter_context(nc.semaphore(name))

        wpq = sb("wpq", [P, 2, P])
        we2 = sb("we2", [P, P])
        w1t = sb("w1t", [P, P])
        be1_bc = sb("be1_bc", [P, P])
        bias1_bc = sb("bias1_bc", [P, P])
        be2_row = sb("be2_row", [1, P])
        bias0_col = sb("bias0_col", [P, 1])
        ident = sb("ident", [P, P])
        ones = sb("ones", [P, 1])
        eps = sb("eps", [P, 1])
        iota_row = sb("iota_row", [P, W])
        iota_col = sb("iota_col", [P, 1])
        iota_win = sb("iota_win", [P, W])
        hT = sb("hT", [P, NPAD])
        xTs = sb("xTs", [P, NPAD])
        aggT = sb("aggT", [P, NPAD])
        cw = sb("cw", [1, 2, NPAD])
        node_a = sb("node_a", [P, TILES, P])
        node_b = sb("node_b", [P, TILES, P])
        x1 = sb("x1", [P, TILES, P])
        deg = sb("deg", [P, TILES])
        dmask = sb("dmask", [P, TILES])
        dtmp = sb("dtmp", [P, TILES])
        dinv = sb("dinv", [P, TILES])
        stats = sb("stats", [P, TILES, 6])
        mv = sb("mv", [P, TILES, 2])
        std = sb("std", [P, TILES])
        rstd = sb("rstd", [P, TILES])
        dsts = sb("dsts", [P, NG * CH], i32)
        ws = sb("ws", [P, NG * CH])
        drel = sb("drel", [P, NG * CH])
        cmin = sb("cmin", [NG, CH])
        cmax = sb("cmax", [NG, CH])
        cspan = sb("cspan", [NG, CH])
        cint = sb("cint", [NG, CH], i32)
        bmin = sb("bmin", [NG, 1])
        bmax = sb("bmax", [NG, 1])
        spans = sb("spans", [NG, 2])
        bint = sb("bint", [NG, 1], i32)
        base_row = sb("base_row", [1, NG], i32)
        base_bc = sb("base_bc", [P, NG], i32)
        base_p = sb("base_p", [P, NG])
        span_row = sb("span_row", [1, 2 * NG])
        span_max = sb("span_max", [1, 2])
        fits = sb("fits", [1, 2])
        scratch = sb("scratch", [1, 1])
        flag = sb("flag", [1, 2], i32)
        lo = sb("lo", [P, NG * CH])
        key = sb("key", [P, NG * CH])
        mcol = sb("mcol", [CH * CW, NG])
        lane = sb("lane", [P, 1], i32)
        lane_hi = sb("lane_hi", [P, 1], i32)
        lane_lo = sb("lane_lo", [P, 1], i32)
        lane_hif = sb("lane_hif", [P, 1])
        lane_lof = sb("lane_lof", [P, 1])
        mine = sb("mine", [CH * CW, CH])
        wp = sb("wp", [P, 3, NG * CH])
        iota_key = sb("iota_key", [P, KEYS], bf16)
        iota_lo = sb("iota_lo", [P, P], bf16)
        khot = [sb(f"khot{s}", [P, CH, KEYS], bf16) for s in range(2)]
        adj = [sb(f"adj{s}", [P, HI, CH * CW]) for s in range(2)]
        part = sb("part", [P, CH * CW])
        partT = sb("partT", [CH * CW, P])
        mrg = [sb(f"mrg{s}", [CH * CW, W]) for s in range(E_TURN)]
        idx = [sb(f"idx{s}", [P, CH], i32) for s in range(2)]
        dbc = [sb(f"dbc{s}", [W, GE], i32) for s in range(2)]
        lhs = [sb(f"lhs{s}", [W + CE, GE]) for s in range(2)]
        rhs = [sb(f"rhs{s}", [W + CE, P]) for s in range(2)]
        gat = [sb(f"gat{s}", [P, CH, P]) for s in range(2)]
        msg = [sb(f"msg{s}", [P, CH, P]) for s in range(2)]
        hot = [sb(f"hot{s}", [P, CH, 2, W]) for s in range(2)]
        idxd = sb("idxd", [P, CH], i32)
        gatq = sb("gatq", [P, CH, P])
        flat = [hT, xTs]
        low = [flat[s][:, 0:CH * 3 * P // 2].bitcast(bf16).rearrange("p (c j k) -> p c j k", c=CH, j=3)
               for s in range(2)]
        lowhot = [msg[s][:, 0:CH // 2, :].rearrange("p c f -> p (c f)").bitcast(bf16)
                  .rearrange("p (c k) -> p c k", c=CH) for s in range(2)]
        x1_flat = x1[:, :, :].rearrange("p t f -> p (t f)")
        srcs = x1_flat[:, 0:NG * CH].bitcast(i32)
        src_hi = x1_flat[:, NG * CH:2 * NG * CH].bitcast(i32)
        cbase = x1_flat[:, 2 * NG * CH:3 * NG * CH].bitcast(i32)
        dgrp = node_a[0:NG, 0:CH, :].bitcast(i32)
        dreal = node_a[0:NG, CH:2 * CH, :]
        w_left = node_b[:, 0:7, :].rearrange("p t f -> p (t f)")[:, 0:NG * CH]
        w_part = node_b[:, 7:14, :].rearrange("p t f -> p (t f)")[:, 0:NG * CH // 2].bitcast(bf16)
        picked = x1_flat[0:CH * CW, 3 * NG * CH:4 * NG * CH]

        ps = ctx.enter_context(nc.psum_tensor("ps", [P, 8, 512], f32))

        def ps_pre(s, h):
            return ps[:, 2 * s + h, :]

        def ps_agg(s):
            return ps[:, 4 + s, 0:W]

        def ps_cw(s):
            return ps[0:1, 6 + s, 0:2 * W]

        const_in = sem("const_in")
        meta_in = sem("meta_in")
        grp_in = sem("grp_in")
        x_in = sem("x_in")
        base_out = sem("base_out")
        base_in = sem("base_in")
        pool_const = sem("pool_const")
        dve_const = sem("dve_const")
        bounds = sem("bounds")
        flag_ready = sem("flag_ready")
        rel_ready = sem("rel_ready")
        rhs_const = [sem(f"rhs_const{s}") for s in range(2)]
        pq_mm = sem("pq_mm")
        p_copied = sem("p_copied")
        q_copied = sem("q_copied")
        p_out = sem("p_out")
        q_out = sem("q_out")
        m_mm = sem("m_mm")
        m_added = sem("m_added")
        agg_clear = sem("agg_clear")
        idx_in = [sem(f"idx_in{s}") for s in range(2)]
        dbc_in = [sem(f"dbc_in{s}") for s in range(2)]
        ea_in = [sem(f"ea_in{s}") for s in range(2)]
        qw_in = [sem(f"qw_in{s}") for s in range(2)]
        rows_in = [[sem(f"rows_in{s}{h}") for h in range(2)] for s in range(2)]
        passed = sem("passed")
        oht_made = sem("oht_made")
        hot_made = sem("hot_made")
        hotw_made = sem("hotw_made")
        pre_mm = sem("pre_mm")
        pre_added = sem("pre_added")
        relu_done = sem("relu_done")
        scat_mm = sem("scat_mm")
        agg_added = sem("agg_added")
        chunk_ready = sem("chunk_ready")
        w_split = sem("w_split")
        ehot_made = sem("ehot_made")
        low_made = sem("low_made")
        adj_mm = sem("adj_mm")
        adj_copied = sem("adj_copied")
        part_mm = sem("part_mm")
        part_copied = sem("part_copied")
        partT_mm = sem("partT_mm")
        partT_copied = sem("partT_copied")
        merge_mm = sem("merge_mm")
        phot_made = sem("phot_made")
        photw_made = sem("photw_made")
        pscat_mm = sem("pscat_mm")
        sums_added = sem("sums_added")
        g_idx = sem("g_idx")
        g_ea = sem("g_ea")
        g_qw = sem("g_qw")
        g_idxd = sem("g_idxd")
        g_rows = sem("g_rows")
        g_rowsq = sem("g_rowsq")
        g_lhs = sem("g_lhs")
        g_pre = sem("g_pre")
        g_add = sem("g_add")
        g_relu = sem("g_relu")
        g_win = sem("g_win")
        g_hot = sem("g_hot")
        g_scat = sem("g_scat")
        g_agg = sem("g_agg")
        g_group = sem("g_group")
        u_ready = sem("u_ready")
        deg_mm = sem("deg_mm")
        dchain = sem("dchain")
        u_tr = sem("u_tr")
        u_copied = sem("u_copied")
        ln_stats = sem("ln_stats")
        ln_var = sem("ln_var")
        ln_std = sem("ln_std")
        ln_rstd = sem("ln_rstd")
        x1_made = sem("x1_made")
        z_made = sem("z_made")
        z_out = sem("z_out")
        z_tr = sem("z_tr")
        z_copied = sem("z_copied")
        x2_made = sem("x2_made")
        y_mm = sem("y_mm")
        y_scaled = sem("y_scaled")
        y_made = sem("y_made")
        out_made = sem("out_made")
        out_out = sem("out_out")

        block = ctx.enter_context(nc.Block())

        def nth(p, g):
            return p * NG + g

        def groups(eng, step):
            step(0, 0, 1, True)
            step(1, 1, 1, True)
            with eng.Fori(1, PAIRS) as j:
                step(2 * j, 0, j + 1, False)
                step(2 * j + 1, 1, j + 1, False)
            step(NG - 1, 0, PAIRS + 1, False)

        def used(p, s, k):
            return p * (PAIRS + (1 if s == 0 else 0)) + k

        def turns(eng, step):
            def turn(i):
                e, q = 0, 0
                for at, kind in enumerate(TURN):
                    step(i, at, i * len(TURN) + at, i * P_TURN + q if kind == "P" else i * E_TURN + e)
                    e, q = e + (kind == "E"), q + (kind == "P")
            turn(0)
            with eng.Fori(1, TURNS) as i:
                turn(i)

        def early(i, at):
            n = TURN[:at].count(TURN[at])
            return type(i) is int and i == 0 and n < (E_LAG if TURN[at] == "E" else P_LAG)

        def adds(i, at):
            if type(i) is int and i == 0:
                return sum(not early(0, a) for a in range(at + 1))
            return i * len(TURN) + (at + 1 - E_LAG - P_LAG)

        def adds_by_next(i, at):
            nxt = TURN.find(TURN[at], at + 1)
            return adds(i, nxt) if nxt >= 0 else adds(i + 1, TURN.find(TURN[at]))

        def place(kind, n):
            return [a for a, k in enumerate(TURN) if k == kind][n]

        def used3(i, at):
            r = TURN[:at].count("P")
            return 2 * (PAIRS + (1 if r % 2 == 0 else 0)) + i * (P_TURN // 2) + r // 2 + 1
        LAST_USE = 2 * (PAIRS + 1) + P_LAST // 2 + 1

        @block.sync
        def _(sp):
            sp.dma_start(dgrp, dst_row.rearrange("(g c p) -> g c p", c=CH, p=P)).then_inc(grp_in, 16)
            sp.dma_start(hT[:, 0:NODES], xT).then_inc(x_in, 16)
            sp.dma_start(wpq[:, :, :], We1[0:2 * P, :].rearrange("(a f) n -> f a n", a=2)).then_inc(const_in, 16)
            sp.dma_start(we2[:, :], We2).then_inc(const_in, 16)
            sp.dma_start(w1t[:, :], W1T).then_inc(const_in, 16)
            sp.dma_start(be1_bc[:, :], be1.rearrange("(a n) -> a n", a=1).to_broadcast([P, P])).then_inc(const_in, 16)
            sp.dma_start(bias1_bc[:, :], bias1.rearrange("(a n) -> a n", a=1).to_broadcast([P, P])).then_inc(const_in, 16)
            sp.dma_start(be2_row[:, :], be2.rearrange("(a n) -> a n", a=1)).then_inc(const_in, 16)
            sp.dma_start(bias0_col[:, :], bias0.rearrange("(n a) -> n a", a=1)).then_inc(const_in, 16)
            for s in range(2):
                sp.dma_start(rhs[s][W:W + CE, :], We1[2 * P:2 * P + CE, :]).then_inc(rhs_const[s], 16)
            sp.dma_start(xTs[:, 0:NODES], xT).then_inc(x_in, 16)
            sp.dma_start(dsts[:, :], dst_em).then_inc(meta_in, 16)
            sp.dma_start(ws[:, :], w_em).then_inc(meta_in, 16)
            sp.dma_start(srcs, src_em).then_inc(meta_in, 16)
            sp.wait_ge(bounds, 10)
            sp.dma_start(base_dram.rearrange("(n a) -> n a", a=1), bint[:, :]).then_inc(base_out, 16)
            sp.dma_start(span_dram.rearrange("(n a) -> n a", a=2), spans[:, :]).then_inc(base_out, 16)
            sp.dma_start(cbase_dram.rearrange("(n a) -> n a", a=CH), cint[:, :]).then_inc(base_out, 16)
            sp.wait_ge(base_out, 48)
            brow = base_dram.rearrange("(a n) -> a n", a=1)
            sp.dma_start(base_row[:, :], brow).then_inc(base_in, 16)
            sp.dma_start(base_bc[:, :], brow.to_broadcast([P, NG])).then_inc(base_in, 16)
            sp.dma_start(span_row[:, :], span_dram.rearrange("(a n) -> a n", a=1)).then_inc(base_in, 16)
            sp.dma_start(cbase, cbase_dram.rearrange("(a n) -> a n", a=1).to_broadcast([P, NG * CH])).then_inc(base_in, 16)
            sp.wait_ge(base_in, 64)
            sp.wait_ge(flag_ready, 1)
            fast = sp.value_load(flag[0:1, 0:1], min_val=0, max_val=1)
            fast3 = sp.value_load(flag[0:1, 1:2], min_val=0, max_val=1)

            for p in range(3):
                if p < 2:
                    for q, (t0, n) in enumerate(QUADS):
                        pairs = 13 * p + (t0 + n) // 2
                        sp.wait_ge(p_copied, pairs)
                        sp.dma_start(p_dram.rearrange("(t p) f -> p t f", p=P)[:, t0:t0 + n, :],
                                     node_a[:, t0:t0 + n, :]).then_inc(p_out, 16)
                        sp.wait_ge(q_copied, pairs)
                        sp.dma_start(q_dram.rearrange("(t p) f -> p t f", p=P)[:, t0:t0 + n, :],
                                     node_b[:, t0:t0 + n, :]).then_inc(q_out, 16)
                    sp.wait_ge(q_out, 16 * len(QUADS) * (p + 1))
                else:
                    for q, (t0, n) in enumerate(QUADS):
                        sp.wait_ge(z_made, t0 + n)
                        sp.dma_start(z_dram.rearrange("(t p) f -> p t f", p=P)[:, t0:t0 + n, :],
                                     node_b[:, t0:t0 + n, :]).then_inc(z_out, 16)
                with sp.If((fast if p < 2 else fast3) == 1):
                    def load(g, s, k, first):
                        old = p > 0 or not first
                        if old:
                            sp.wait_ge(rows_in[s][1], 16 * HALF * (used(p, s, k) - 1))
                        sp.dma_start(idx[s][:, :], src_g[bass.ds(g, 1), :, :].rearrange("a p k -> (a p) k")
                                     ).then_inc(idx_in[s], 16)
                        if old:
                            sp.wait_ge(oht_made, nth(p, g) - 1)
                        row = dst_row[bass.ds(g * GE, GE)].rearrange("(a n) -> a n", a=1)
                        sp.dma_start(dbc[s][:, :], row.to_broadcast([W, GE])).then_inc(dbc_in[s], 16)
                        if old:
                            sp.wait_ge(pre_mm, 2 * (nth(p, g) - 1))
                        sp.dma_start(lhs[s][W:W + CE, :], eaT[:, bass.ds(g * GE, GE)]).then_inc(ea_in[s], 16)
                        sp.sem_inc(passed, 1)
                        b = sp.value_load(base_row[0:1, bass.ds(g, 1)], min_val=0, max_val=NODES - 1)
                        sp.dma_start(rhs[s][0:W, :], q_dram[bass.ds(b, W), :]).then_inc(qw_in[s], 16)

                    def load3(i, at, g, n):
                        if TURN[at] == "E":
                            return
                        slot = TURN[:at].count("P") % 2
                        sp.wait_ge(rows_in[slot][1], 16 * HALF * (used3(i, at) - 1))
                        sp.dma_start(idx[slot][:, :], src_g[bass.ds(g, 1), :, :].rearrange("a p k -> (a p) k")
                                     ).then_inc(idx_in[slot], 16)
                    if p < 2:
                        groups(sp, load)
                    else:
                        turns(sp, load3)
                        sp.wait_ge(rows_in[0][1], 16 * HALF * (LAST_USE - 1))
                        sp.dma_start(idx[0][:, :], src_g[NG - 1, :, :]).then_inc(idx_in[0], 16)
                with sp.Else():
                    with sp.Fori(0, NG) as g:
                        sp.wait_ge(g_group, nth(p, g) + 1)
                        sp.dma_start(idx[0][:, :], src_g[bass.ds(g, 1), :, :].rearrange("a p k -> (a p) k")
                                     ).then_inc(g_idx, 16)
                        if p < 2:
                            sp.dma_start(lhs[0][W:W + CE, :], eaT[:, bass.ds(g * GE, GE)]).then_inc(g_ea, 16)
                            sp.dma_start(rhs[0][0:W, :], q_dram[0:W, :]).then_inc(g_qw, 16)
            for q, (t0, n) in enumerate(QUADS):
                sp.wait_ge(out_made, t0 + n)
                full = min(n, FULL - t0)
                sp.dma_start(out[t0 * P:(t0 + full) * P, :].rearrange("(t p) f -> p t f", p=P) if full > 0 else
                             out[FULL * P:NODES, :],
                             node_b[:, t0:t0 + full, :] if full > 0 else node_b[0:REST, FULL, :]).then_inc(out_out, 16)
            sp.wait_ge(out_out, 16 * len(QUADS))
            sp.wait_ge(p_out, 32 * len(QUADS))
            sp.wait_ge(q_out, 32 * len(QUADS))
            sp.wait_ge(z_out, 16 * len(QUADS))

        @block.gpsimd
        def _(pool):
            pool.iota(iota_row[:, :], pattern=[[1, W]], base=0, channel_multiplier=0,
                      allow_small_or_imprecise_dtypes=True).then_inc(pool_const, 1)
            pool.iota(iota_col[:, :], pattern=[[0, 1]], base=0, channel_multiplier=1,
                      allow_small_or_imprecise_dtypes=True).then_inc(pool_const, 1)
            pool.memset(ident[:, :], 0.0).then_inc(pool_const, 1)
            pool.iota(lane[:, :], pattern=[[0, 1]], base=0, channel_multiplier=1).then_inc(pool_const, 1)
            pool.iota(iota_key[:, :], pattern=[[1, KEYS]], base=0, channel_multiplier=0,
                      allow_small_or_imprecise_dtypes=True).then_inc(pool_const, 1)
            pool.iota(iota_lo[:, :], pattern=[[1, P]], base=0, channel_multiplier=0,
                      allow_small_or_imprecise_dtypes=True).then_inc(pool_const, 1)
            pool.wait_ge(pool_const, 6)
            pool.affine_select(out=ident[:, :], in_=ident[:, :], compare_op=ALU.not_equal, fill=1.0,
                               base=0, pattern=[[-1, P]], channel_multiplier=1).then_inc(pool_const, 1)
            pool.wait_ge(flag_ready, 1)
            fast = pool.value_load(flag[0:1, 0:1], min_val=0, max_val=1)
            fast3 = pool.value_load(flag[0:1, 1:2], min_val=0, max_val=1)

            def rows(out_, table, index):
                return pool.indirect_dma_start(out=out_, out_offset=None, in_=table,
                                               in_offset=bass.IndirectOffsetOnAxis(ap=index, axis=0))
            for p in range(3):
                table = p_dram if p < 2 else z_dram
                if p < 2:
                    pool.wait_ge(p_out, 16 * len(QUADS) * (p + 1))
                else:
                    pool.wait_ge(z_out, 16 * len(QUADS))
                with pool.If((fast if p < 2 else fast3) == 1):
                    def gather(g, s, k, first):
                        pool.wait_ge(idx_in[s], 16 * used(p, s, k))
                        for h in range(2):
                            if p > 0 or not first:
                                pool.wait_ge(pre_added, 2 * (nth(p, g) - 2) + h + 1)
                            pool.sem_inc(passed, 1)
                            for c in range(h * HALF, (h + 1) * HALF):
                                rows(gat[s][:, c, :], table, idx[s][:, c:c + 1]).then_inc(rows_in[s][h], 16)

                    def gather3(slot, use, scattered):
                        pool.wait_ge(idx_in[slot], 16 * use)
                        if scattered is not None:
                            pool.wait_ge(pscat_mm, scattered)
                        pool.sem_inc(passed, 1)
                        for c in range(CH):
                            rows(gat[slot][:, c, :], table, idx[slot][:, c:c + 1]).then_inc(rows_in[slot][c // HALF], 16)

                    def step3(i, at, g, n):
                        if TURN[at] == "P":
                            gather3(TURN[:at].count("P") % 2, used3(i, at),
                                    None if type(i) is int and n < 2 else n - 1)
                    if p < 2:
                        groups(pool, gather)
                    else:
                        turns(pool, step3)
                        gather3(0, LAST_USE, P_LAST - 1)
                with pool.Else():
                    with pool.Fori(0, NG) as g:
                        pool.wait_ge(g_idx, 16 * (nth(p, g) + 1))
                        pool.sem_inc(passed, 1)
                        for c in range(CH):
                            rows(gat[0][:, c, :], table, idx[0][:, c:c + 1]).then_inc(g_rows, 16)
                        if p < 2:
                            pool.wait_ge(g_idxd, nth(p, g) + 1)
                            pool.sem_inc(passed, 1)
                            for c in range(CH):
                                rows(gatq[:, c, :], q_dram, idxd[:, c:c + 1]).then_inc(g_rowsq, 16)

        @block.tensor
        def _(pe):
            pe.wait_ge(flag_ready, 1)
            fast = pe.value_load(flag[0:1, 0:1], min_val=0, max_val=1)
            fast3 = pe.value_load(flag[0:1, 1:2], min_val=0, max_val=1)
            pe.wait_ge(const_in, 16 * 7)
            pe.wait_ge(pool_const, 7)
            pe.wait_ge(dve_const, 5)
            for s in range(2):
                pe.wait_ge(rhs_const[s], 16)
            pe.wait_ge(x_in, 32)

            def pre_products(s, h):
                for c in range(h * HALF, (h + 1) * HALF):
                    last = nc.tensor.matmul(ps_pre(s, h)[:, (c % HALF) * P:(c % HALF + 1) * P],
                                            lhs[s][:, c * P:(c + 1) * P], rhs[s][:, :], start=True, stop=True)
                return last

            def scatter_products(p, s):
                if p == 0:
                    for c in range(CH):
                        nc.tensor.matmul(ps_cw(s), ones[:, 0:1], hot[s][:, c, :, :].rearrange("p a w -> p (a w)"),
                                         start=(c == 0), stop=(c == CH - 1))
                for c in range(CH):
                    last = nc.tensor.matmul(ps_agg(s), (msg if p < 2 else gat)[s][:, c, :],
                                            hot[s][:, c, (0 if p < 2 else 1), :], start=(c == 0), stop=(c == CH - 1))
                return last

            for p in range(3):
                if p < 2:
                    for t in range(TILES):
                        pair = 13 * p + t // 2
                        if p:
                            pe.wait_ge(m_added, NBLK * (p - 1) + -(-(t + 1) * P // BLK))
                        if t % 2 == 0 and t >= 4:
                            pe.wait_ge(p_copied, pair - 1)
                            pe.wait_ge(q_copied, pair - 1)
                        for a in range(2):
                            mm = nc.tensor.matmul(ps[:, 2 * (t // 2 % 2) + a, (t % 2) * P:(t % 2 + 1) * P],
                                                  hT[:, t * P:(t + 1) * P], wpq[:, a, :], start=True, stop=True)
                        if t % 2:
                            mm.then_inc(pq_mm, 1)
                    pe.wait_ge(p_copied, 13 * (p + 1))
                    pe.wait_ge(q_copied, 13 * (p + 1))
                with pe.If((fast if p < 2 else fast3) == 1):
                    def products(g, s, k, first):
                        n = nth(p, g)
                        if True:
                            pe.wait_ge(oht_made, n + 1)
                            pe.wait_ge(ea_in[s], 16 * used(p, s, k))
                            pe.wait_ge(qw_in[s], 16 * used(p, s, k))
                            for h in range(2):
                                if p > 0 or not first:
                                    pe.wait_ge(pre_added, 2 * (n - 2) + h + 1)
                                pre_products(s, h).then_inc(pre_mm, 1)
                            pe.wait_ge(relu_done, 2 * n + 2)
                        if p == 0:
                            pe.wait_ge(hotw_made, g + 1)
                        else:
                            pe.wait_ge(hot_made, n + 1)
                        if p > 0 or not first:
                            pe.wait_ge(agg_added, n - 1)
                        scatter_products(p, s).then_inc(scat_mm, 1)

                    def adjacency(q, slot, first):
                        pe.wait_ge(ehot_made, q + 1)
                        pe.wait_ge(low_made, q + 1)
                        for b in range(CH // 2):
                            if not first:
                                pe.wait_ge(adj_copied, (q - 1) * (CH // 2) + b + 1)
                            for c in (2 * b, 2 * b + 1):
                                for w in range(3):
                                    mm = nc.tensor.matmul(ps[:, b, (c % 2) * KEYS:(c % 2 + 1) * KEYS],
                                                          low[slot][:, c, w, :], khot[slot][:, c, :],
                                                          start=(w == 0), stop=(w == 2))
                            mm.then_inc(adj_mm, 1)

                    def block_sums(q, slot, first):
                        pe.wait_ge(adj_copied, (q + 1) * (CH // 2))
                        if not first:
                            pe.wait_ge(part_copied, q)
                        for t in range(HI):
                            mm = nc.tensor.matmul(ps[:, 6, 0:CH * CW], node_b[:, t, :], adj[slot][:, t, :],
                                                  start=(t == 0), stop=(t == HI - 1))
                        mm.then_inc(part_mm, 1)

                    def turn_sums(q, added):
                        pe.wait_ge(part_copied, q + 1)
                        if added is not None:
                            pe.wait_ge(sums_added, added)
                        pe.sem_inc(passed, 1)
                        nc.tensor.transpose(ps[0:CH * CW, 7, 0:P], part[:, :], ident[:, :]).then_inc(partT_mm, 1)

                    def merge_sums(q, slot):
                        pe.wait_ge(partT_copied, q + 1)
                        nc.tensor.matmul(ps[:, 7, 0:W], partT[:, :], mrg[slot][:, :], start=True, stop=True
                                         ).then_inc(merge_mm, 1)

                    def scatter3(m, slot, use, added):
                        for h in range(2):
                            pe.wait_ge(rows_in[slot][h], 16 * HALF * use)
                        pe.wait_ge(photw_made, m + 1)
                        if added is not None:
                            pe.wait_ge(sums_added, added)
                        scatter_products(2, slot).then_inc(pscat_mm, 1)

                    def step3(i, at, g, n):
                        r = TURN[:at].count(TURN[at])
                        start = type(i) is int
                        if TURN[at] == "P":
                            scatter3(n, r % 2, used3(i, at), None if start and r < 2 else adds(i, at))
                            return
                        adjacency(n, r % 2, start and r == 0)
                        if not (start and r < 2):
                            turn_sums(n - 2, None if start and r == 2 else adds_by_next(i, at))
                        if not (start and r < 1):
                            block_sums(n - 1, (r + 1) % 2, start and r == 1)
                        if not (start and r < 2):
                            merge_sums(n - 2, (r - 2) % E_TURN)
                    if p < 2:
                        groups(pe, products)
                    else:
                        turns(pe, step3)
                        done = len(TURN) * TURNS - E_LAG - P_LAG
                        scatter3(P_LAST, 0, LAST_USE, done + 2)
                        block_sums(E_LAST - 1, 1, False)
                        for q in (E_LAST - 2, E_LAST - 1):
                            turn_sums(q, done + (3 if q == E_LAST - 2 else 5))
                            merge_sums(q, q % E_TURN)
                with pe.Else():
                    with pe.Fori(0, NG) as g:
                        n = nth(p, g)
                        if p < 2:
                            pe.wait_ge(g_lhs, n + 1)
                            pe.wait_ge(g_ea, 16 * (n + 1))
                            pe.wait_ge(g_qw, 16 * (n + 1))
                            for h in range(2):
                                last = pre_products(0, h)
                            last.then_inc(g_pre, 1)
                            pe.wait_ge(g_relu, n + 1)
                        else:
                            pe.wait_ge(g_rows, 16 * CH * (n + 1))
                        pe.sem_inc(passed, 1)
                        with pe.Fori(0, NWIN) as w:
                            pe.wait_ge(g_hot, n * NWIN + w + 1)
                            scatter_products(p, 0).then_inc(g_scat, 1)
                if p < 2:
                    pe.wait_ge(agg_clear, 2 * p + 1)
                    for b in range(NBLK):
                        if b >= 4:
                            pe.wait_ge(m_added, NBLK * p + b - 3)
                        cols = slice(b * BLK, (b + 1) * BLK)
                        nc.tensor.matmul(ps[:, 4 + b % 4, 0:BLK], we2[:, :], aggT[:, cols], start=True, stop=False)
                        nc.tensor.matmul(ps[:, 4 + b % 4, 0:BLK], be2_row[:, :], cw[0:1, 0, cols],
                                         start=False, stop=True).then_inc(m_mm, 1)
                if p == 1:
                    pe.wait_ge(m_added, 2 * NBLK)
                    for t in range(TILES):
                        mm = nc.tensor.matmul(ps[:, 7, t:t + 1], cw[0:1, 1, t * P:(t + 1) * P], ones[0:1, 0:1],
                                              start=True, stop=True)
                    mm.then_inc(deg_mm, 1)
                    pe.wait_ge(u_ready, 1)
                    for q, (t0, n) in enumerate(QUADS):
                        if q >= 4:
                            pe.wait_ge(u_copied, q - 3)
                        for t in range(t0, t0 + n):
                            tr = nc.tensor.transpose(ps[:, q % 4, (t - t0) * P:(t - t0 + 1) * P],
                                                     hT[:, t * P:(t + 1) * P], ident[:, :])
                        tr.then_inc(u_tr, 1)
                    pe.wait_ge(u_copied, len(QUADS))
                    for q, (t0, n) in enumerate(QUADS):
                        pe.wait_ge(z_made, t0 + n)
                        if q >= 4:
                            pe.wait_ge(z_copied, q - 3)
                        for t in range(t0, t0 + n):
                            tr = nc.tensor.transpose(ps[:, q % 4, (t - t0) * P:(t - t0 + 1) * P],
                                                     node_b[:, t, :], ident[:, :])
                        tr.then_inc(z_tr, 1)
                    pe.wait_ge(z_copied, len(QUADS))
            pe.wait_ge(agg_clear, 5)
            for q, (t0, n) in enumerate(QUADS):
                if q >= 4:
                    pe.wait_ge(y_scaled, t0 - 12)
                for t in range(t0, t0 + n):
                    mm = nc.tensor.matmul(ps[:, q % 4, (t - t0) * P:(t - t0 + 1) * P],
                                          aggT[:, t * P:(t + 1) * P], w1t[:, :], start=True, stop=True)
                mm.then_inc(y_mm, 1)

        @block.scalar
        def _(act):
            act.wait_ge(flag_ready, 1)
            fast = act.value_load(flag[0:1, 0:1], min_val=0, max_val=1)
            fast3 = act.value_load(flag[0:1, 1:2], min_val=0, max_val=1)
            for p in range(3):
                if p < 2:
                    if p:
                        act.wait_ge(p_out, 16 * len(QUADS))
                    for j in range(TILES // 2):
                        act.wait_ge(pq_mm, 13 * p + j + 1)
                        nc.scalar.copy(node_a[:, 2 * j:2 * j + 2, :],
                                       ps[:, 2 * (j % 2), 0:2 * P].rearrange("p (t f) -> p t f", t=2)
                                       ).then_inc(p_copied, 1)
                    with act.If((fast if p < 2 else fast3) == 1):
                        def relu(g, s, k, first):
                            for h in range(2):
                                act.wait_ge(pre_added, 2 * nth(p, g) + h + 1)
                                m = msg[s][:, h * HALF:(h + 1) * HALF, :]
                                nc.scalar.activation(m, m, ACT.Relu).then_inc(relu_done, 1)
                        groups(act, relu)
                    with act.Else():
                        with act.Fori(0, NG) as g:
                            act.wait_ge(g_add, 2 * nth(p, g) + 2)
                            nc.scalar.activation(msg[0][:, :, :], msg[0][:, :, :], ACT.Relu).then_inc(g_relu, 1)
                if p == 1:
                    act.wait_ge(p_out, 2 * 16 * len(QUADS))
                    for q, (t0, n) in enumerate(QUADS):
                        act.wait_ge(u_tr, q + 1)
                        nc.scalar.copy(node_a[:, t0:t0 + n, :],
                                       ps[:, q % 4, 0:n * P].rearrange("p (t f) -> p t f", f=P)).then_inc(u_copied, 1)
                    act.wait_ge(dchain, 3)
                    nc.scalar.activation(dtmp[:, :], dtmp[:, :], ACT.Sqrt).then_inc(ln_std, 1)
                    act.wait_ge(ln_var, TILES)
                    nc.scalar.activation(std[:, :], mv[:, :, 1], ACT.Sqrt, bias=eps[:, 0:1]).then_inc(ln_std, 1)
                    act.wait_ge(q_out, 2 * 16 * len(QUADS))
                    act.wait_ge(dchain, 5)
                    for t in range(TILES):
                        act.wait_ge(x1_made, t + 1)
                        nc.scalar.mul(node_b[:, t, :], x1[:, t, :], dinv[:, t:t + 1]).then_inc(z_made, 1)
                    for q, (t0, n) in enumerate(QUADS):
                        act.wait_ge(z_tr, q + 1)
                        nc.scalar.copy(aggT[:, t0 * P:(t0 + n) * P], ps[:, q % 4, 0:n * P]).then_inc(z_copied, 1)
            with act.If(fast3 == 1):
                def copy_block(q, slot, first):
                    for b in range(CH // 2):
                        act.wait_ge(adj_mm, q * (CH // 2) + b + 1)
                        if b == 0 and not first:
                            act.wait_ge(part_mm, q - 1)
                        nc.scalar.copy(adj[slot][:, :, 2 * b * CW:2 * (b + 1) * CW].rearrange("p t (c j) -> p c t j", c=2),
                                       ps[:, b, 0:2 * KEYS].rearrange("p (c t j) -> p c t j", c=2, t=HI)
                                       ).then_inc(adj_copied, 1)

                def weigh_low(g, q, slot, first):
                    if not first:
                        act.wait_ge(adj_mm, (q - 1) * (CH // 2))
                    act.wait_ge(ehot_made, q + 1)
                    for c in range(CH):
                        at = bass.ds(g * CH + c, 1)
                        for w in (1, 2):
                            last = nc.scalar.mul(low[slot][:, c, w, :], lowhot[slot][:, c, :], wp[:, w, at])
                    last.then_inc(low_made, 1)

                def copy_sums(q, first):
                    act.wait_ge(part_mm, q + 1)
                    if not first:
                        act.wait_ge(partT_mm, q)
                    nc.scalar.copy(part[:, :], ps[:, 6, 0:CH * CW]).then_inc(part_copied, 1)

                def copy_turned(q, first):
                    act.wait_ge(partT_mm, q + 1)
                    if not first:
                        act.wait_ge(merge_mm, q)
                    nc.scalar.copy(partT[:, :], ps[0:CH * CW, 7, 0:P]).then_inc(partT_copied, 1)

                def step3(i, at, g, n):
                    r = TURN[:at].count(TURN[at])
                    start = type(i) is int
                    if TURN[at] == "P":
                        return
                    if not (start and r < 1):
                        copy_block(n - 1, (r + 1) % 2, start and r < 3)
                    weigh_low(g, n, r % 2, start and r < 2)
                    if not (start and r < 3):
                        copy_turned(n - 3, start and r == 3)
                    if not (start and r < 2):
                        copy_sums(n - 2, start and r == 2)
                turns(act, step3)
                copy_block(E_LAST - 1, 1, False)
                copy_turned(E_LAST - 3, False)
                copy_sums(E_LAST - 2, False)
                copy_turned(E_LAST - 2, False)
                copy_sums(E_LAST - 1, False)
                copy_turned(E_LAST - 1, False)
            act.wait_ge(ln_var, 2 * TILES)
            nc.scalar.activation(std[:, :], mv[:, :, 1], ACT.Sqrt, bias=eps[:, 0:1]).then_inc(ln_std, 1)

        @block.vector
        def _(dve):
            V = nc.vector
            V.memset(ones[:, :], 1.0).then_inc(dve_const, 1)
            V.memset(eps[:, :], EPS).then_inc(dve_const, 1)
            V.memset(aggT[:, :], 0.0).then_inc(dve_const, 1)
            V.memset(cw[:, :, :], 0.0).then_inc(dve_const, 1)
            V.memset(hT[:, NODES:NPAD], 0.0).then_inc(dve_const, 1)
            V.memset(xTs[:, NODES:NPAD], 0.0).then_inc(dve_const, 1)
            dve.wait_ge(grp_in, 16)
            V.tensor_reduce(cmin[:, :], dgrp, AX.X, ALU.min).then_inc(bounds, 1)
            V.scalar_tensor_tensor(dreal, dgrp, float(NODES), dgrp, ALU.is_lt, ALU.mult
                                   ).then_inc(bounds, 1)
            dve.wait_ge(bounds, 2)
            V.tensor_reduce(cmax[:, :], dreal, AX.X, ALU.max).then_inc(bounds, 1)
            V.tensor_reduce(bmin[:, :], cmin[:, :], AX.X, ALU.min).then_inc(bounds, 1)
            V.tensor_copy(cint[:, :], cmin[:, :]).then_inc(bounds, 1)
            dve.wait_ge(bounds, 5)
            V.tensor_reduce(bmax[:, :], cmax[:, :], AX.X, ALU.max).then_inc(bounds, 1)
            V.tensor_tensor(cspan[:, :], cmax[:, :], cmin[:, :], ALU.subtract).then_inc(bounds, 1)
            V.tensor_copy(bint[:, :], bmin[:, :]).then_inc(bounds, 1)
            dve.wait_ge(bounds, 8)
            V.tensor_tensor(spans[:, 0:1], bmax[:, :], bmin[:, :], ALU.subtract).then_inc(bounds, 1)
            V.tensor_reduce(spans[:, 1:2], cspan[:, :], AX.X, ALU.max).then_inc(bounds, 1)
            dve.wait_ge(base_in, 64)
            V.tensor_reduce(span_max[:, :], span_row[:, :].rearrange("a (n k) -> a k n", k=2), AX.X, ALU.max
                            ).then_inc(bounds, 1)
            dve.wait_ge(bounds, 11)
            V.tensor_single_scalar(fits[:, 0:1], span_max[:, 0:1], float(W), ALU.is_lt).then_inc(bounds, 1)
            V.tensor_single_scalar(fits[:, 1:2], span_max[:, 1:2], float(CW), ALU.is_lt).then_inc(bounds, 1)
            dve.wait_ge(bounds, 13)
            V.tensor_copy(flag[:, 0:1], fits[:, 0:1]).then_inc(bounds, 1)
            dve.wait_ge(bounds, 14)
            V.tensor_tensor(flag[:, 1:2], fits[:, 0:1], fits[:, 1:2], ALU.mult).then_inc(flag_ready, 1)
            dve.wait_ge(pool_const, 7)
            V.tensor_scalar(base_p[:, :], base_bc[:, :], iota_col[:, 0:1], None, ALU.add).then_inc(rel_ready, 1)
            dve.wait_ge(meta_in, 48)
            V.tensor_tensor(drel[:, :].rearrange("p (g c) -> p g c", c=CH),
                            dsts[:, :].rearrange("p (g c) -> p g c", c=CH),
                            base_bc[:, :].unsqueeze(2).to_broadcast([P, NG, CH]), ALU.subtract).then_inc(rel_ready, 1)
            dve.wait_ge(flag_ready, 1)
            fast = dve.value_load(flag[0:1, 0:1], min_val=0, max_val=1)
            fast3 = dve.value_load(flag[0:1, 1:2], min_val=0, max_val=1)
            dve.wait_ge(rel_ready, 2)
            dve.wait_ge(dve_const, 6)
            dve.wait_ge(const_in, 16 * 7)

            def chunk_keys():
                R = CH * CW
                V.tensor_single_scalar(src_hi, srcs, 7, ALU.arith_shift_right).then_inc(chunk_ready, 1)
                V.tensor_single_scalar(srcs, srcs, P - 1, ALU.bitwise_and).then_inc(chunk_ready, 1)
                V.tensor_tensor(key[:, :], dsts[:, :], cbase, ALU.subtract).then_inc(chunk_ready, 1)
                V.tensor_single_scalar(lane_hi[:, :], lane[:, :], CW.bit_length() - 1, ALU.arith_shift_right
                                       ).then_inc(chunk_ready, 1)
                V.tensor_single_scalar(lane_lo[:, :], lane[:, :], CW - 1, ALU.bitwise_and).then_inc(chunk_ready, 1)
                dve.wait_ge(chunk_ready, 5)
                V.tensor_copy(lo[:, :], srcs).then_inc(chunk_ready, 1)
                V.scalar_tensor_tensor(key[:, :], src_hi, float(CW), key[:, :], ALU.mult, ALU.add
                                       ).then_inc(chunk_ready, 1)
                V.tensor_copy(lane_hif[:, :], lane_hi[:, :]).then_inc(chunk_ready, 1)
                V.tensor_copy(lane_lof[:, :], lane_lo[:, :]).then_inc(chunk_ready, 1)
                dve.wait_ge(chunk_ready, 9)
                V.tensor_scalar(mine[:, :], iota_row[0:R, 0:CH], lane_hif[0:R, 0:1], None, ALU.is_equal
                                ).then_inc(chunk_ready, 1)
                dve.wait_ge(chunk_ready, 10)
                V.tensor_tensor(picked.rearrange("r (g c) -> r g c", c=CH), cbase[0:R, :].rearrange("r (g c) -> r g c", c=CH),
                                mine[:, :].unsqueeze(1).to_broadcast([R, NG, CH]), ALU.mult).then_inc(chunk_ready, 1)
                dve.wait_ge(chunk_ready, 11)
                V.tensor_reduce(mcol[:, :], picked.rearrange("r (g c) -> r g c", c=CH), AX.X, ALU.add
                                ).then_inc(chunk_ready, 1)
                dve.wait_ge(chunk_ready, 12)
                V.scalar_tensor_tensor(mcol[:, :], mcol[:, :], lane_lof[0:R, 0:1], base_bc[0:R, :], ALU.add, ALU.subtract
                                       ).then_inc(chunk_ready, 1)

            def one_hot(s, ids, window):
                return V.tensor_tensor(hot[s][:, :, 0, :], window[:, :].unsqueeze(1).to_broadcast([P, CH, W]),
                                       ids.unsqueeze(2).to_broadcast([P, CH, W]), ALU.is_equal)

            def weigh(s, g):
                return V.tensor_tensor(hot[s][:, :, 1, :], hot[s][:, :, 0, :],
                                       ws[:, bass.ds(g * CH, CH)].unsqueeze(2).to_broadcast([P, CH, W]), ALU.mult)

            def fast_steps(eng, vector_step, add_window, p):
                vector_step(0, 0, 1, True, before=False)
                vector_step(1, 1, 1, True)
                with eng.Fori(1, PAIRS) as j:
                    vector_step(2 * j, 0, j + 1, False)
                    vector_step(2 * j + 1, 1, j + 1, False)
                vector_step(NG - 1, 0, PAIRS + 1, False)
                eng.wait_ge(agg_added, nth(p, NG - 1))
                add_window(NG - 1, 0)
                eng.wait_ge(agg_added, nth(p, NG))

            left = ws[:, :]
            for w in range(3):
                V.tensor_copy(w_part, left).then_inc(w_split, 1)
                dve.wait_ge(w_split, 3 * w + 1)
                V.tensor_copy(wp[:, w, :], w_part).then_inc(w_split, 1)
                dve.wait_ge(w_split, 3 * w + 2)
                V.tensor_tensor(w_left, left, wp[:, w, :], ALU.subtract).then_inc(w_split, 1)
                dve.wait_ge(w_split, 3 * w + 3)
                left = w_left

            for p in range(3):
                if p < 2:
                    if p:
                        dve.wait_ge(q_out, 16 * len(QUADS))
                    for j in range(TILES // 2):
                        dve.wait_ge(pq_mm, 13 * p + j + 1)
                        V.tensor_tensor(node_b[:, 2 * j:2 * j + 2, :],
                                        ps[:, 2 * (j % 2) + 1, 0:2 * P].rearrange("p (t f) -> p t f", t=2),
                                        be1_bc[:, :].unsqueeze(1).to_broadcast([P, 2, P]), ALU.add
                                        ).then_inc(q_copied, 1)
                    if p == 0:
                        chunk_keys()
                else:
                    dve.wait_ge(z_copied, len(QUADS))
                    dve.wait_ge(chunk_ready, 13)
                with dve.If((fast if p < 2 else fast3) == 1):
                    def add_window(g, s):
                        n = nth(p, g)
                        dve.sem_inc(passed, 1)
                        b = dve.value_load(base_row[0:1, bass.ds(g, 1)], min_val=0, max_val=NODES - 1)
                        dve.wait_ge(scat_mm, n + 1)
                        if p == 0:
                            c = cw[0:1, :, bass.ds(b, W)]
                            V.tensor_tensor(c, c, ps_cw(s).rearrange("p (a w) -> p a w", a=2), ALU.add)
                        a = aggT[:, bass.ds(b, W)]
                        V.tensor_tensor(a, a, ps_agg(s), ALU.add).then_inc(agg_added, 1)

                    def vector_step(g, s, k, first, before=True):
                        n = nth(p, g)
                        old = p > 0 or not first
                        dve.wait_ge(dbc_in[s], 16 * used(p, s, k))
                        if old:
                            dve.wait_ge(pre_mm, 2 * (n - 1))
                        V.tensor_scalar(lhs[s][0:W, :], dbc[s][:, :], base_p[0:W, bass.ds(g, 1)], None,
                                        ALU.is_equal).then_inc(oht_made, 1)
                        if old:
                            dve.wait_ge(scat_mm, n - 1)
                        one_hot(s, drel[:, bass.ds(g * CH, CH)], iota_row).then_inc(hot_made, 1)
                        if p == 0:
                            dve.wait_ge(hot_made, n + 1)
                            weigh(s, g).then_inc(hotw_made, 1)
                        if before:
                            if old:
                                dve.wait_ge(agg_added, n - 1)
                            add_window(g - 1, 1 - s)
                        for h in range(2):
                            dve.wait_ge(rows_in[s][h], 16 * HALF * used(p, s, k))
                            dve.wait_ge(pre_mm, 2 * n + h + 1)
                            V.tensor_tensor(msg[s][:, h * HALF:(h + 1) * HALF, :],
                                            ps_pre(s, h).rearrange("p (c f) -> p c f", f=P),
                                            gat[s][:, h * HALF:(h + 1) * HALF, :], ALU.add).then_inc(pre_added, 1)

                    def add_sums(kind, g, n, bank, before):
                        dve.sem_inc(passed, 1)
                        b = dve.value_load(base_row[0:1, bass.ds(g, 1)], min_val=0, max_val=NODES - 1)
                        dve.wait_ge(merge_mm if kind == "E" else pscat_mm, n + 1)
                        if before is not None:
                            dve.wait_ge(sums_added, before)
                        a = aggT[:, bass.ds(b, W)]
                        V.tensor_tensor(a, a, ps[:, bank, 0:W], ALU.add).then_inc(sums_added, 1)

                    def e_hots(g, q, r, first, start):
                        if not first:
                            dve.wait_ge(adj_mm, (q - 1) * (CH // 2))
                        if not start:
                            dve.wait_ge(merge_mm, q - E_TURN + 1)
                        V.tensor_scalar(mrg[r][:, :], iota_row[0:CH * CW, :], mcol[:, bass.ds(g, 1)], None,
                                        ALU.is_equal)
                        for c in range(CH):
                            at = bass.ds(g * CH + c, 1)
                            V.tensor_scalar(khot[r % 2][:, c, :], iota_key[:, :], key[:, at], None, ALU.is_equal)
                            V.tensor_scalar(low[r % 2][:, c, 0, :], iota_lo[:, :], lo[:, at], wp[:, 0, at],
                                            ALU.is_equal, ALU.mult)
                            last = V.tensor_scalar(lowhot[r % 2][:, c, :], iota_lo[:, :], lo[:, at], None,
                                                   ALU.is_equal)
                        last.then_inc(ehot_made, 1)

                    def p_hots(g, m, slot, first):
                        if not first:
                            dve.wait_ge(pscat_mm, m - 1)
                        one_hot(slot, drel[:, bass.ds(g * CH, CH)], iota_row).then_inc(phot_made, 1)
                        dve.wait_ge(phot_made, m + 1)
                        weigh(slot, g).then_inc(photw_made, 1)

                    def back(kind, r, at):
                        r -= E_LAG if kind == "E" else P_LAG
                        per = E_TURN if kind == "E" else P_TURN
                        return at - place(kind, r) if r >= 0 else at + len(TURN) - place(kind, r + per)

                    def step3(i, at, g, n):
                        r = TURN[:at].count(TURN[at])
                        start = type(i) is int
                        count = adds(i, at) - 1
                        if start and count < 1:
                            count = None
                        if TURN[at] == "P":
                            p_hots(g, n, r % 2, start and r < 2)
                            if not early(i, at):
                                add_sums("P", g - back("P", r, at), n - P_LAG, 4 + r % 2, count)
                        else:
                            e_hots(g, n, r, start and r < 2, start)
                            if not early(i, at):
                                add_sums("E", g - back("E", r, at), n - E_LAG, 7, count)

                    if p == 2:
                        turns(dve, step3)
                        p_hots(NG - 1, P_LAST, 0, False)
                        done = len(TURN) * TURNS - E_LAG - P_LAG
                        for kind, n in (("E", E_LAST - 4), ("P", P_LAST - 2), ("E", E_LAST - 3), ("P", P_LAST - 1),
                                        ("E", E_LAST - 2), ("P", P_LAST), ("E", E_LAST - 1)):
                            per = E_TURN if kind == "E" else P_TURN
                            g = NG - 1 if (kind, n) == ("P", P_LAST) else n // per * len(TURN) + place(kind, n % per)
                            add_sums(kind, g, n, 7 if kind == "E" else 4 + n % 2, done)
                            done += 1
                        dve.wait_ge(sums_added, done)
                    if p < 2:
                        fast_steps(dve, vector_step, add_window, p)
                    V.memset(scratch[:, :], 0.0).then_inc(agg_clear, 1)
                with dve.Else():
                    if p == 0:
                        V.memset(lhs[0][0:W, :], 0.0).then_inc(g_group, 1)
                    with dve.Fori(0, NG) as g:
                        n = nth(p, g)
                        dve.wait_ge(g_group, n + 1)
                        if p < 2:
                            V.tensor_single_scalar(idxd[:, :], dsts[:, bass.ds(g * CH, CH)], float(NPAD - 1),
                                                   ALU.min).then_inc(g_idxd, 1)
                            V.memset(iota_win[:, :], 0.0).then_inc(g_lhs, 1)
                            dve.wait_ge(g_rows, 16 * CH * (n + 1))
                            dve.wait_ge(g_pre, n + 1)
                            V.tensor_tensor(msg[0][:, :, :], ps[:, 0:2, :].rearrange("p h (c f) -> p (h c) f", f=P),
                                            gat[0][:, :, :], ALU.add).then_inc(g_add, 1)
                            dve.wait_ge(g_rowsq, 16 * CH * (n + 1))
                            dve.wait_ge(g_add, 2 * n + 1)
                            V.tensor_tensor(msg[0][:, :, :], msg[0][:, :, :], gatq[:, :, :], ALU.add
                                            ).then_inc(g_add, 1)
                            dve.wait_ge(g_add, 2 * n + 2)
                        V.tensor_copy(iota_win[:, :], iota_row[:, :]).then_inc(g_win, 1)
                        with dve.Fori(0, NWIN) as w:
                            m = n * NWIN + w
                            dve.wait_ge(g_win, n * (NWIN + 1) + w + 1)
                            one_hot(0, dsts[:, bass.ds(g * CH, CH)], iota_win).then_inc(hot_made, 1)
                            dve.wait_ge(hot_made, m + 1)
                            weigh(0, g).then_inc(g_hot, 1)
                            V.tensor_scalar_add(iota_win[:, :], iota_win[:, :], float(W)).then_inc(g_win, 1)
                            dve.wait_ge(g_scat, m + 1)
                            if p == 0:
                                V.tensor_tensor(cw[0:1, :, bass.ds(w * W, W)], cw[0:1, :, bass.ds(w * W, W)],
                                                ps_cw(0).rearrange("p (a w) -> p a w", a=2), ALU.add)
                            V.tensor_tensor(aggT[:, bass.ds(w * W, W)], aggT[:, bass.ds(w * W, W)], ps_agg(0),
                                            ALU.add).then_inc(g_agg, 1)
                            dve.wait_ge(g_agg, m + 1)
                        V.memset(scratch[:, :], 0.0).then_inc(g_group, 1)
                    dve.wait_ge(g_group, nth(p, NG) + 1)
                    V.memset(scratch[:, :], 0.0).then_inc(agg_clear, 1)
                if p < 2:
                    for b in range(NBLK):
                        cols = slice(b * BLK, (b + 1) * BLK)
                        dve.wait_ge(m_mm, NBLK * p + b + 1)
                        V.tensor_tensor(hT[:, cols], hT[:, cols], ps[:, 4 + b % 4, 0:BLK], ALU.add).then_inc(m_added, 1)
                    dve.wait_ge(agg_clear, 2 * p + 1)
                    V.memset(aggT[:, :], 0.0).then_inc(agg_clear, 1)
                    dve.wait_ge(agg_clear, 2 * p + 2)
                if p == 1:
                    dve.wait_ge(m_added, 2 * NBLK)
                    V.scalar_tensor_tensor(hT[:, :], hT[:, :], bias0_col[:, 0:1], xTs[:, :], ALU.add, ALU.add
                                           ).then_inc(u_ready, 1)
                    dve.wait_ge(deg_mm, 1)
                    V.tensor_scalar_add(deg[:, :], ps[:, 7, 0:TILES], 1.0).then_inc(dchain, 1)
                    dve.wait_ge(dchain, 1)
                    V.tensor_single_scalar(dmask[:, :], deg[:, :], 0.0, ALU.is_gt).then_inc(dchain, 1)
                    dve.wait_ge(dchain, 2)
                    V.tensor_copy(dtmp[:, :], ones[:, 0:1].to_broadcast([P, TILES])).then_inc(bounds, 1)
                    dve.wait_ge(bounds, 15)
                    V.copy_predicated(dtmp[:, :], dmask[:, :].bitcast(mybir.dt.uint32), deg[:, :]).then_inc(dchain, 1)
                    dve.wait_ge(ln_std, 1)
                    V.reciprocal(dtmp[:, :], dtmp[:, :]).then_inc(dchain, 1)
                    dve.wait_ge(dchain, 4)
                    V.tensor_tensor(dinv[:, :], dtmp[:, :], dmask[:, :], ALU.mult).then_inc(dchain, 1)

                def layer_norm(which, src, made, dst):
                    for t in range(TILES):
                        made(t)
                        V.bn_stats(stats[:, t, :], src[:, t, :]).then_inc(ln_stats, 1)
                    for t in range(TILES):
                        dve.wait_ge(ln_stats, which * TILES + t + 1)
                        V.bn_aggr(mv[:, t, :], stats[:, t, :]).then_inc(ln_var, 1)
                    dve.wait_ge(ln_std, which + 2)
                    V.reciprocal(rstd[:, :], std[:, :]).then_inc(ln_rstd, 1)
                    dve.wait_ge(ln_rstd, which + 1)
                    for t in range(TILES):
                        V.tensor_scalar(dst[:, t, :], src[:, t, :], mv[:, t, 0:1], rstd[:, t:t + 1],
                                        ALU.subtract, ALU.mult).then_inc(x1_made if which == 0 else out_made, 1)

                if p == 1:
                    layer_norm(0, node_a, lambda t: dve.wait_ge(u_copied, t // 4 + 1), x1)
                    dve.wait_ge(x1_made, TILES)
                    dve.wait_ge(z_made, TILES)
                    V.tensor_scalar_mul(x1[:, :, :], x1[:, :, :], 2.0).then_inc(x2_made, 1)
            dve.wait_ge(x2_made, 1)
            for t in range(TILES):
                dve.wait_ge(y_mm, t // 4 + 1)
                V.scalar_tensor_tensor(node_a[:, t, :], ps[:, (t // 4) % 4, (t % 4) * P:(t % 4 + 1) * P],
                                       dinv[:, t:t + 1], bias1_bc[:, :], ALU.mult, ALU.add).then_inc(y_scaled, 1)
                dve.wait_ge(y_scaled, t + 1)
                V.scalar_tensor_tensor(node_a[:, t, :], node_a[:, t, :], 0.0, x1[:, t, :], ALU.max, ALU.add
                                       ).then_inc(y_made, 1)
            dve.wait_ge(z_out, 16 * len(QUADS))
            layer_norm(1, node_a, lambda t: dve.wait_ge(y_made, t + 1), node_b)


def kernel(**inputs):
    import numpy as np
    import concourse.bacc as bacc
    from concourse.bass_utils import run_bass_kernel_spmd

    f32, i32 = mybir.dt.float32, mybir.dt.int32
    pad = NG * GE - EDGES
    src = np.concatenate([np.asarray(inputs["src"]), np.zeros(pad, np.int32)])
    dst = np.concatenate([np.asarray(inputs["dst"]), np.full(pad, OFF, np.int32)])
    ew = np.concatenate([np.asarray(inputs["edge_weight"]), np.zeros(pad, np.float32)])
    ea = np.concatenate([np.asarray(inputs["edge_attr_32"]), np.zeros((pad, CE), np.float32)])
    by_lane = lambda a: np.ascontiguousarray(a.reshape(NG * CH, P).T)
    arrays = {
        "xT": np.ascontiguousarray(np.asarray(inputs["x"]).T),
        "src_g": np.ascontiguousarray(src.reshape(NG, CH, P).transpose(0, 2, 1)),
        "src_em": by_lane(src), "dst_row": dst, "dst_em": by_lane(dst), "w_em": by_lane(ew),
        "eaT": np.ascontiguousarray(ea.T),
        "We1": np.asarray(inputs["L0_gnn_We1"]), "be1": np.asarray(inputs["L0_gnn_be1"]),
        "We2": np.asarray(inputs["L0_gnn_We2"]), "be2": np.asarray(inputs["L0_gnn_be2"]),
        "bias0": np.asarray(inputs["L0_gnn_bias"]),
        "W1T": np.ascontiguousarray(np.asarray(inputs["L1_gnn_weight"]).T),
        "bias1": np.asarray(inputs["L1_gnn_bias"]),
    }
    nc = bacc.Bacc("TRN2", target_bir_lowering=False, num_devices=1)
    args = {n: nc.dram_tensor(n, a.shape, mybir.dt.from_np(a.dtype), kind="ExternalInput").ap()
            for n, a in arrays.items()}
    out = nc.dram_tensor("out", (NODES, P), f32, kind="ExternalOutput").ap()
    scratch = {n: nc.dram_tensor(n, (NPAD, P), f32, kind="Internal").ap() for n in ("p_dram", "q_dram", "z_dram")}
    build(nc, out=out, base_dram=nc.dram_tensor("base_dram", (NG,), i32, kind="Internal").ap(),
          cbase_dram=nc.dram_tensor("cbase_dram", (NG * CH,), i32, kind="Internal").ap(),
          span_dram=nc.dram_tensor("span_dram", (2 * NG,), f32, kind="Internal").ap(), **scratch, **args)
    r = run_bass_kernel_spmd(nc, [arrays], core_ids=[0])
    return r.results[0]["out"]
```

```python
import concourse.bass as bass
from concourse import mybir
from contextlib import ExitStack

P = 128
NODES = 3125
EDGES = 103125
CE = 32
TILES = 26
NPAD = TILES * P
CH = 8
HALF = CH // 2
GE = CH * P
NG = -(-EDGES // GE)
PAIRS = (NG - 1) // 2
STRETCH = 10
STRETCHES = (NG - 1) // STRETCH
WHOLE = [STRETCHES + 1, 1]
W = 64
CW = 8
HI = -(-NODES // P)
MID = HI * P // 2
KEYS = HI * CW
NWIN = -(-NODES // W)
OFF = 8191
BLK = 2 * P
NBLK = NPAD // BLK
EPS = 1e-5
TURN = "EPPEPEP" * 2
SIZE = {"E": 2, "P": 1}


def groups_in(items):
    return sum(SIZE[kind] for kind in items)


TG = groups_in(TURN)
TURNS = NG // TG
E_TURN, P_TURN = TURN.count("E"), TURN.count("P")
E_LAST = E_TURN * TURNS
P_LAST = P_TURN * TURNS
E_LAG, P_LAG = 3, 2
DIRECT = 1
QUADS = [(q, min(4, TILES - q)) for q in range(0, TILES, 4)]
PIECES = [(t, min(7, TILES - t)) for t in range(0, TILES, 7)]
OUT_ACT = [t for t in range(1, 20, 2)]
OUT_DVE = [t for t in range(TILES) if t not in OUT_ACT]
OUTS = [(0, 1), (1, 1), (2, 2)] + QUADS[1:]
FULL = NODES // P
REST = NODES - FULL * P


def build(nc, xT, src_g, src_em, src_row, dst_row, dst_em, w_em, eaT, We1, be1, We2, be2, bias0, W1T, bias1,
          out, p_dram, q_dram, z_dram, base_dram, span_dram, cbase_dram):
    f32, bf16, f16, i32 = mybir.dt.float32, mybir.dt.bfloat16, mybir.dt.float16, mybir.dt.int32
    ALU, ACT, AX = mybir.AluOpType, mybir.ActivationFunctionType, mybir.AxisListType
    ctx = ExitStack()
    with ctx:
        def sb(name, shape, dt=f32):
            return ctx.enter_context(nc.sbuf_tensor(name, shape, dt))

        def sem(name):
            return ctx.enter_context(nc.semaphore(name))

        wpq = sb("wpq", [P, 2, P])
        we2 = sb("we2", [P, P])
        w1t = sb("w1t", [P, P])
        be1_bc = sb("be1_bc", [P, P])
        bias1_bc = sb("bias1_bc", [P, P])
        be2_row = sb("be2_row", [4, P])
        parts = sb("parts", [4, 1])
        bias0_col = sb("bias0_col", [P, 1])
        ident = sb("ident", [P, P])
        ones = sb("ones", [P, 1])
        eps = sb("eps", [P, 1])
        iota_row = sb("iota_row", [P, W])
        iota_col = sb("iota_col", [P, 1])
        iota_win = sb("iota_win", [P, W])
        hT = sb("hT", [P, NPAD])
        xTs = sb("xTs", [P, NPAD])
        aggT = sb("aggT", [P, NPAD])
        cw = sb("cw", [4, NPAD])
        node_a = sb("node_a", [P, TILES, P])
        node_b = sb("node_b", [P, TILES, P])
        x1 = sb("x1", [P, TILES, P])
        deg = sb("deg", [P, TILES])
        dmask = sb("dmask", [P, TILES])
        dtmp = sb("dtmp", [P, TILES])
        dinv = sb("dinv", [P, TILES])
        stats = sb("stats", [P, TILES, 6])
        mv = sb("mv", [P, TILES, 2])
        std = sb("std", [P, TILES])
        rstd = sb("rstd", [P, TILES])
        zscale = sb("zscale", [P, TILES])
        zshift = sb("zshift", [P, TILES])
        xscale = sb("xscale", [P, TILES])
        xshift = sb("xshift", [P, TILES])
        dsts = sb("dsts", [P, NG * CH], i32)
        ws = sb("ws", [P, NG * CH])
        drel = sb("drel", [P, NG * CH])
        cmin = sb("cmin", [NG, CH])
        cmax = sb("cmax", [NG, CH])
        cspan = sb("cspan", [NG, CH])
        cint = sb("cint", [NG, CH], i32)
        bmin = sb("bmin", [NG, 1])
        bmax = sb("bmax", [NG, 1])
        spans = sb("spans", [NG, 2])
        bint = sb("bint", [NG, 1], i32)
        base_row = sb("base_row", [1, NG], i32)
        base_bc = sb("base_bc", [P, NG], i32)
        base_p = sb("base_p", [P, NG])
        span_row = sb("span_row", [1, 2 * NG])
        span_max = sb("span_max", [1, 2])
        fits = sb("fits", [1, 2])
        scratch = sb("scratch", [1, 1])
        flag = sb("flag", [1, 1], i32)
        lo = sb("lo", [P, NG * CH])
        key = sb("key", [P, NG * CH])
        mcol = sb("mcol", [P, NG])
        lane = sb("lane", [P, 1], i32)
        lane_hi = sb("lane_hi", [P, 1], i32)
        lane_lo = sb("lane_lo", [P, 1], i32)
        lane_hif = sb("lane_hif", [P, 1])
        lane_lof = sb("lane_lof", [P, 1])
        mine = sb("mine", [P, CH])
        wp = sb("wp", [P, 3, NG * CH])
        iota_key = sb("iota_key", [P, KEYS], bf16)
        iota_lo = sb("iota_lo", [P, P], bf16)
        khots = sb("khots", [P, 2, CH, KEYS], bf16)
        khot = [khots[:, s, :, :] for s in range(2)]
        adj = sb("adj", [P, HI, 2 * CH * CW])
        part = sb("part", [P, 2 * CH * CW])
        partT = sb("partT", [2 * CH * CW, P])
        mrg = [sb(f"mrg{s}", [2 * CH * CW, 2 * W]) for s in range(3)]
        idx = [sb(f"idx{s}", [P, CH], i32) for s in range(2)]
        dbc = [sb(f"dbc{s}", [W, GE], i32) for s in range(2)]
        lhs = [sb(f"lhs{s}", [W + CE, GE]) for s in range(2)]
        rhs = [sb(f"rhs{s}", [W + CE, P]) for s in range(2)]
        gat = [sb(f"gat{s}", [P, CH, P]) for s in range(2)]
        msg = [sb(f"msg{s}", [P, CH, P]) for s in range(2)]
        hot = [sb(f"hot{s}", [P, CH, 2, W]) for s in range(2)]
        tally = [sb(f"tally{s}", [P, CH, 4], bf16) for s in range(2)]
        sbc = [sb(f"sbc{s}", [P, P], i32) for s in range(2)]
        sbc16 = sb("sbc16", [P, P], f16)
        idxd = sb("idxd", [P, CH], i32)
        gatq = sb("gatq", [P, CH, P])
        flat = [hT, xTs]
        adj_flat = adj[:, :, :].rearrange("p t k -> p (t k)")
        p_part = [a[:, 0:HI * P // 2] for a in (x1[:, :, :].rearrange("p t f -> p (t f)"),
                                                x1[:, :, :].rearrange("p t f -> p (t f)")[:, HI * P // 2:],
                                                adj_flat)]
        p_part = [a.bitcast(bf16).rearrange("p (t f) -> p t f", t=HI) for a in p_part]
        shot = [adj_flat[:, HI * P // 2:],
                node_a[:, :, :].rearrange("p t f -> p (t f)")[:, 0:HI * P // 2]]
        shot = [a.bitcast(bf16).rearrange("p (t e) -> p t e", t=HI) for a in shot]
        numbers = khots[:, :, :, :].rearrange("p s c k -> p (s c k)").bitcast(f16).rearrange("p (t e) -> p t e", t=HI)
        blocks = [adj[:, :, :], node_a[:, 0:HI, :]]
        rest = node_b
        low = [flat[s][:, 0:CH * 3 * P // 2].bitcast(bf16).rearrange("p (c j k) -> p c j k", c=CH, j=3)
               for s in range(2)]
        lowhot = [msg[s][:, 0:CH // 2, :].rearrange("p c f -> p (c f)").bitcast(bf16)
                  .rearrange("p (c k) -> p c k", c=CH) for s in range(2)]
        xTs_flat = xTs[:, :]
        srcs = xTs_flat[:, 0:NG * CH].bitcast(i32)
        src_hi = xTs_flat[:, NG * CH:2 * NG * CH].bitcast(i32)
        cbase = xTs_flat[:, 2 * NG * CH:3 * NG * CH].bitcast(i32)
        picked = xTs_flat[:, 3 * NG * CH:4 * NG * CH]
        dgrp = gat[0][0:NG, :, :].bitcast(i32)
        dreal = gat[1][0:NG, :, :]
        w_left = gatq[:, :, :].rearrange("p c f -> p (c f)")[:, 0:NG * CH]
        hot_flat = [hot[s][:, :, :, :].rearrange("p c j w -> p (c j w)").bitcast(bf16) for s in range(2)]
        w_part = [hot_flat[1][:, 0:NG * CH], hot_flat[1][:, NG * CH:2 * NG * CH], hot_flat[0][:, 0:NG * CH]]

        ps = ctx.enter_context(nc.psum_tensor("ps", [P, 8, 512], f32))

        def hot_bf(s):
            return hot[s][:, :, 1, :].bitcast(bf16)[:, :, 0:W]

        def ps_pre(s, h):
            return ps[:, 2 * s + h, :]

        def ps_agg(s):
            return ps[:, 4 + s, 0:W]

        def ps_cw(s):
            return ps[0:4, 6 + s, 0:W]

        const_in = sem("const_in")
        meta_in = sem("meta_in")
        grp_in = sem("grp_in")
        x_in = [sem(f"x_in{i}") for i in range(len(PIECES))]
        xs_in = sem("xs_in")
        wpq_in = sem("wpq_in")
        be1_in = sem("be1_in")
        base_out = sem("base_out")
        base_in = sem("base_in")
        pool_const = sem("pool_const")
        dve_const = sem("dve_const")
        bounds = sem("bounds")
        flag_ready = sem("flag_ready")
        rel_ready = sem("rel_ready")
        rhs_const = [sem(f"rhs_const{s}") for s in range(2)]
        p_mm = sem("p_mm")
        q_mm = sem("q_mm")
        p_copied = sem("p_copied")
        q_copied = sem("q_copied")
        p_out = sem("p_out")
        q_out = sem("q_out")
        m_mm = sem("m_mm")
        cb_mm = sem("cb_mm")
        cb_added = sem("cb_added")
        x_joined = sem("x_joined")
        m_added = sem("m_added")
        agg_clear = sem("agg_clear")
        idx_in = [sem(f"idx_in{s}") for s in range(2)]
        dbc_in = [sem(f"dbc_in{s}") for s in range(2)]
        ea_in = [sem(f"ea_in{s}") for s in range(2)]
        qw_in = [sem(f"qw_in{s}") for s in range(2)]
        rows_in = [[sem(f"rows_in{s}{h}") for h in range(2)] for s in range(2)]
        passed = sem("passed")
        oht_made = sem("oht_made")
        hot_made = sem("hot_made")
        hotw_made = sem("hotw_made")
        pre_mm = sem("pre_mm")
        pre_added = sem("pre_added")
        relu_done = sem("relu_done")
        scat_mm = sem("scat_mm")
        agg_added = sem("agg_added")
        chunk_ready = sem("chunk_ready")
        w_split = sem("w_split")
        w_kept = sem("w_kept")
        sbc_in = [sem(f"sbc_in{s}") for s in range(2)]
        sbc_cut = sem("sbc_cut")
        shot_made = sem("shot_made")
        part_cut = sem("part_cut")
        part_left = sem("part_left")
        ehot_made = sem("ehot_made")
        low_made = sem("low_made")
        adj_mm = sem("adj_mm")
        adj_copied = sem("adj_copied")
        part_mm = sem("part_mm")
        part_copied = sem("part_copied")
        partT_mm = sem("partT_mm")
        partT_copied = sem("partT_copied")
        merge_mm = sem("merge_mm")
        mrg_made = sem("mrg_made")
        mrg_clear = sem("mrg_clear")
        phot_made = sem("phot_made")
        photw_made = sem("photw_made")
        pscat_mm = sem("pscat_mm")
        sums_added = sem("sums_added")
        g_idx = sem("g_idx")
        g_ea = sem("g_ea")
        g_qw = sem("g_qw")
        g_idxd = sem("g_idxd")
        g_rows = sem("g_rows")
        g_rowsq = sem("g_rowsq")
        g_lhs = sem("g_lhs")
        g_pre = sem("g_pre")
        g_add = sem("g_add")
        g_relu = sem("g_relu")
        g_win = sem("g_win")
        g_hot = sem("g_hot")
        g_scat = sem("g_scat")
        g_agg = sem("g_agg")
        g_group = sem("g_group")
        deg_mm = sem("deg_mm")
        dchain = sem("dchain")
        u_tr = sem("u_tr")
        u_copied = sem("u_copied")
        ln_stats = sem("ln_stats")
        ln_var = sem("ln_var")
        ln_std = sem("ln_std")
        ln_rstd = sem("ln_rstd")
        ln_scale = sem("ln_scale")
        z_even = sem("z_even")
        z_odd = sem("z_odd")
        x_even = sem("x_even")
        x_odd = sem("x_odd")
        z_out = sem("z_out")
        z_tr = sem("z_tr")
        z_copied = sem("z_copied")
        y_mm = sem("y_mm")
        y_scaled = sem("y_scaled")
        y_made = sem("y_made")
        out_dve = sem("out_dve")
        out_act = sem("out_act")
        out_out = sem("out_out")

        block = ctx.enter_context(nc.Block())

        def again(p, g):
            return p > 0 or type(g) is not int or g >= 2

        def nth(p, g):
            return p * NG + g

        def rows_of(s, h, use, whole):
            return 16 * HALF * use if h == 0 else 16 * (HALF - 1) * use + 16 * whole

        def rows_of3(s, h, i, at, back=0):
            uses = 2 * (PAIRS + (1 if s == 0 else 0))
            r = P_TURN if at is None else TURN[:at].count("P")
            return i * (16 * HALF * P_TURN // 2) + (rows_of(s, h, uses, 2 * WHOLE[s]) + 16 * HALF * (r // 2 + 1 - back))

        def groups(eng, step):
            def pair(i, j, own, own_next):
                g, k = i * STRETCH + j * 2, i * (STRETCH // 2) + j + 1
                first = type(g) is int and g == 0
                step(g, 0, k, first, i + 1, own, not first)
                step(g + 1, 1, k, first, 1, not first, own_next)

            def stretch(i):
                pair(i, 0, False, True)
                with eng.Fori(1, STRETCH // 2 - 1) as j:
                    pair(i, j, True, True)
                pair(i, STRETCH // 2 - 1, True, False)
            stretch(0)
            with eng.Fori(1, STRETCHES) as i:
                stretch(i)
            step(NG - 1, 0, PAIRS + 1, False, WHOLE[0], False, False)

        def used(p, s, k):
            return p * (PAIRS + (1 if s == 0 else 0)) + k

        def turns(eng, step):
            def turn(i):
                for at, kind in enumerate(TURN):
                    step(i, at, i * TG + groups_in(TURN[:at]),
                         i * TURN.count(kind) + TURN[:at].count(kind))
            turn(0)
            with eng.Fori(1, TURNS) as i:
                turn(i)

        def early(i, at):
            n = TURN[:at].count(TURN[at])
            return type(i) is int and i == 0 and n < (E_LAG if TURN[at] == "E" else P_LAG)

        def adds(i, at):
            if type(i) is int and i == 0:
                return sum(SIZE[TURN[a]] for a in range(at + 1) if not early(0, a))
            return i * TG + (groups_in(TURN[:at + 1]) - 2 * E_LAG - P_LAG)

        def place(kind, n):
            return [a for a, k in enumerate(TURN) if k == kind][n]

        def used3(i, at):
            r = TURN[:at].count("P")
            return 2 * (PAIRS + (1 if r % 2 == 0 else 0)) + i * (P_TURN // 2) + r // 2 + 1

        LAST_USE = 2 * (PAIRS + 1) + P_LAST // 2 + 1

        @block.sync
        def _(sp):
            sp.dma_start(dgrp, dst_row.rearrange("(g c p) -> g c p", c=CH, p=P)).then_inc(grp_in, 16)
            sp.dma_start(wpq[:, :, :], We1[0:2 * P, :].rearrange("(a f) n -> f a n", a=2)).then_inc(wpq_in, 16)
            for i in range(0, len(PIECES), 2):
                cols = slice(PIECES[i][0] * P, min(sum(PIECES[i]) * P, NODES))
                sp.dma_start(hT[:, cols], xT[:, cols]).then_inc(x_in[i], 16)
            sp.dma_start(be1_bc[:, :], be1.rearrange("(a n) -> a n", a=1).to_broadcast([P, P])).then_inc(be1_in, 16)
            sp.dma_start(dsts[:, :], dst_em).then_inc(meta_in, 16)
            sp.wait_ge(bounds, 10)
            sp.dma_start(base_dram.rearrange("(n a) -> n a", a=1), bint[:, :]).then_inc(base_out, 16)
            sp.dma_start(span_dram.rearrange("(n a) -> n a", a=2), spans[:, :]).then_inc(base_out, 16)
            sp.dma_start(cbase_dram.rearrange("(n a) -> n a", a=CH), cint[:, :]).then_inc(base_out, 16)
            sp.dma_start(ws[:, :], w_em).then_inc(meta_in, 16)
            sp.dma_start(srcs, src_em).then_inc(meta_in, 16)
            sp.wait_ge(base_out, 48)
            brow = base_dram.rearrange("(a n) -> a n", a=1)
            sp.dma_start(base_row[:, :], brow).then_inc(base_in, 16)
            sp.dma_start(base_bc[:, :], brow.to_broadcast([P, NG])).then_inc(base_in, 16)
            sp.dma_start(span_row[:, :], span_dram.rearrange("(a n) -> a n", a=1)).then_inc(base_in, 16)
            sp.dma_start(cbase, cbase_dram.rearrange("(a n) -> a n", a=1).to_broadcast([P, NG * CH])
                         ).then_inc(base_in, 16)
            sp.dma_start(bias0_col[:, :], bias0.rearrange("(n a) -> n a", a=1)).then_inc(const_in, 16)
            for s in range(2):
                sp.dma_start(rhs[s][W:W + CE, :], We1[2 * P:2 * P + CE, :]).then_inc(rhs_const[s], 16)
            sp.wait_ge(flag_ready, 1)
            fast = sp.value_load(flag[0:1, 0:1], min_val=0, max_val=1)

            for p in range(3):
                if p < 2:
                    sp.wait_ge(p_copied, 13 * (p + 1))
                    for s in range(2):
                        sp.dma_start(idx[s][:, :], src_g[s, :, :]).then_inc(idx_in[s], 16)
                    for q, (t0, n) in enumerate(QUADS):
                        sp.wait_ge(q_copied, 13 * p + (t0 + n) // 2)
                        sp.dma_start(q_dram.rearrange("(t p) f -> p t f", p=P)[:, t0:t0 + n, :],
                                     node_b[:, t0:t0 + n, :]).then_inc(q_out, 16)
                else:
                    for q, (t0, n) in enumerate(QUADS):
                        sp.wait_ge(z_even, (t0 + n) // 2)
                        sp.wait_ge(z_odd, (t0 + n) // 2)
                        sp.dma_start(z_dram.rearrange("(t p) f -> p t f", p=P)[:, t0:t0 + n, :],
                                     node_b[:, t0:t0 + n, :]).then_inc(z_out, 16)
                if p == 0:
                    sp.dma_start(be2_row[0:1, :], be2.rearrange("(a n) -> a n", a=1)).then_inc(const_in, 16)
                    sp.dma_start(we2[:, :], We2).then_inc(const_in, 16)
                    sp.dma_start(w1t[:, :], W1T).then_inc(const_in, 16)
                    sp.dma_start(bias1_bc[:, :], bias1.rearrange("(a n) -> a n", a=1).to_broadcast([P, P])
                                 ).then_inc(const_in, 16)
                with sp.If(fast == 1):
                    def load(g, s, k, first, whole, own, own_next):
                        old = p > 0 or not first
                        if old:
                            sp.wait_ge(rows_in[s][1], rows_of(s, 1, used(p, s, k) - 1,
                                                             p * WHOLE[s] + whole - (0 if own else 1)))
                        if not first:
                            sp.dma_start(idx[s][:, :], src_g[bass.ds(g, 1), :, :].rearrange("a p k -> (a p) k")
                                         ).then_inc(idx_in[s], 16)
                        if old:
                            sp.wait_ge(oht_made, nth(p, g) - 1)
                        row = dst_row[bass.ds(g * GE, GE)].rearrange("(a n) -> a n", a=1)
                        sp.dma_start(dbc[s][:, :], row.to_broadcast([W, GE])).then_inc(dbc_in[s], 16)
                        if old:
                            sp.wait_ge(sbc_cut, nth(p, g) - 1)
                        row = src_row[bass.ds(g * GE + GE - P, P)].rearrange("(a n) -> a n", a=1)
                        sp.dma_start(sbc[s][:, :], row.to_broadcast([P, P])).then_inc(sbc_in[s], 16)
                        if old:
                            sp.wait_ge(pre_mm, 2 * (nth(p, g) - 1))
                        sp.dma_start(lhs[s][W:W + CE, :], eaT[:, bass.ds(g * GE, GE)]).then_inc(ea_in[s], 16)
                        if type(g) is int and g == 0:
                            sp.wait_ge(q_out, 16 * len(QUADS) * (p + 1))
                        sp.sem_inc(passed, 1)
                        b = sp.value_load(base_row[0:1, bass.ds(g, 1)], min_val=0, max_val=NODES - 1)
                        sp.dma_start(rhs[s][0:W, :], q_dram[bass.ds(b, W), :]).then_inc(qw_in[s], 16)

                    def load3(i, at, g, n):
                        if TURN[at] == "E":
                            return
                        slot = TURN[:at].count("P") % 2
                        sp.wait_ge(rows_in[slot][1], rows_of3(slot, 1, i, at, back=1))
                        sp.dma_start(idx[slot][:, :], src_g[bass.ds(g, 1), :, :].rearrange("a p k -> (a p) k")
                                     ).then_inc(idx_in[slot], 16)
                    if p < 2:
                        groups(sp, load)
                    else:
                        turns(sp, load3)
                        sp.wait_ge(rows_in[0][1], rows_of3(0, 1, TURNS - 1, None, back=1))
                        sp.dma_start(idx[0][:, :], src_g[NG - 1, :, :]).then_inc(idx_in[0], 16)
                with sp.Else():
                    sp.wait_ge(q_out, 16 * len(QUADS) * (min(p, 1) + 1))
                    sp.wait_ge(idx_in[0], 16 * (min(p, 1) + 1))
                    with sp.Fori(0, NG) as g:
                        sp.wait_ge(g_group, nth(p, g) + 1)
                        sp.dma_start(idx[0][:, :], src_g[bass.ds(g, 1), :, :].rearrange("a p k -> (a p) k")
                                     ).then_inc(g_idx, 16)
                        if p < 2:
                            sp.dma_start(lhs[0][W:W + CE, :], eaT[:, bass.ds(g * GE, GE)]).then_inc(g_ea, 16)
                            sp.dma_start(rhs[0][0:W, :], q_dram[0:W, :]).then_inc(g_qw, 16)
                if p == 0:
                    sp.wait_ge(chunk_ready, 14)
                    sp.dma_start(xTs[:, 0:NODES], xT).then_inc(xs_in, 16)
            for t0, n in OUTS:
                sp.wait_ge(out_dve, sum(t < t0 + n for t in OUT_DVE))
                sp.wait_ge(out_act, sum(t < t0 + n for t in OUT_ACT))
                full = min(n, FULL - t0)
                sp.dma_start(out[t0 * P:(t0 + full) * P, :].rearrange("(t p) f -> p t f", p=P) if full > 0 else
                             out[FULL * P:NODES, :],
                             node_b[:, t0:t0 + full, :] if full > 0 else node_b[0:REST, FULL, :]).then_inc(out_out, 16)
            sp.wait_ge(out_out, 16 * len(OUTS))
            sp.wait_ge(p_out, 32 * len(QUADS))
            sp.wait_ge(q_out, 32 * len(QUADS))
            sp.wait_ge(z_out, 16 * len(QUADS))

        @block.gpsimd
        def _(pool):
            pool.iota(iota_row[:, :], pattern=[[1, W]], base=0, channel_multiplier=0,
                      allow_small_or_imprecise_dtypes=True).then_inc(pool_const, 1)
            pool.iota(iota_col[:, :], pattern=[[0, 1]], base=0, channel_multiplier=1,
                      allow_small_or_imprecise_dtypes=True).then_inc(pool_const, 1)
            pool.memset(ident[:, :], 0.0).then_inc(pool_const, 1)
            pool.iota(lane[:, :], pattern=[[0, 1]], base=0, channel_multiplier=1).then_inc(pool_const, 1)
            pool.iota(iota_key[:, :], pattern=[[1, KEYS]], base=0, channel_multiplier=0,
                      allow_small_or_imprecise_dtypes=True).then_inc(pool_const, 1)
            pool.iota(iota_lo[:, :], pattern=[[1, P]], base=0, channel_multiplier=0,
                      allow_small_or_imprecise_dtypes=True).then_inc(pool_const, 1)
            pool.iota(numbers, pattern=[[P, HI], [0, P]], base=-MID, channel_multiplier=1,
                      allow_small_or_imprecise_dtypes=True).then_inc(pool_const, 1)
            pool.memset(cw[:, :], 0.0).then_inc(pool_const, 1)
            pool.memset(aggT[:, :], 0.0).then_inc(pool_const, 1)
            pool.wait_ge(pool_const, 9)
            pool.affine_select(out=ident[:, :], in_=ident[:, :], compare_op=ALU.not_equal, fill=1.0,
                               base=0, pattern=[[-1, P]], channel_multiplier=1).then_inc(pool_const, 1)
            pool.wait_ge(flag_ready, 1)
            fast = pool.value_load(flag[0:1, 0:1], min_val=0, max_val=1)

            def rows(out_, table, index):
                return pool.indirect_dma_start(out=out_, out_offset=None, in_=table,
                                               in_offset=bass.IndirectOffsetOnAxis(ap=index, axis=0))
            for p in range(3):
                table = p_dram if p < 2 else z_dram
                if p < 2:
                    pool.wait_ge(p_out, 16 * len(QUADS) * (p + 1))
                else:
                    pool.wait_ge(z_out, 16 * len(QUADS))
                with pool.If(fast == 1):
                    def gather(g, s, k, first, whole, own, own_next):
                        pool.wait_ge(idx_in[s], 16 * used(p, s, k))
                        for h in range(2):
                            if p > 0 or not first:
                                pool.wait_ge(pre_added, 2 * (nth(p, g) - 2) + h + 1)
                            pool.sem_inc(passed, 1)
                            for c in range(h * HALF, min((h + 1) * HALF, CH - 1 if own else CH)):
                                rows(gat[s][:, c, :], table, idx[s][:, c:c + 1]).then_inc(rows_in[s][h], 16)

                    def gather3(slot, use, scattered):
                        pool.wait_ge(idx_in[slot], 16 * use)
                        if scattered is not None:
                            pool.wait_ge(pscat_mm, scattered)
                        pool.sem_inc(passed, 1)
                        for c in range(CH):
                            rows(gat[slot][:, c, :], table, idx[slot][:, c:c + 1]
                                 ).then_inc(rows_in[slot][c // HALF], 16)

                    def step3(i, at, g, n):
                        if TURN[at] == "P":
                            gather3(TURN[:at].count("P") % 2, used3(i, at),
                                    None if type(i) is int and n < 2 else n - 1)
                    if p < 2:
                        groups(pool, gather)
                    else:
                        turns(pool, step3)
                        gather3(0, LAST_USE, P_LAST - 1)
                with pool.Else():
                    with pool.Fori(0, NG) as g:
                        pool.wait_ge(g_idx, 16 * (nth(p, g) + 1))
                        pool.sem_inc(passed, 1)
                        for c in range(CH):
                            rows(gat[0][:, c, :], table, idx[0][:, c:c + 1]).then_inc(g_rows, 16)
                        if p < 2:
                            pool.wait_ge(g_idxd, nth(p, g) + 1)
                            pool.sem_inc(passed, 1)
                            for c in range(CH):
                                rows(gatq[:, c, :], q_dram, idxd[:, c:c + 1]).then_inc(g_rowsq, 16)
                if p == 0:
                    pool.wait_ge(m_mm, NBLK)
                    pool.memset(aggT[:, :], 0.0).then_inc(agg_clear, 1)

        @block.tensor
        def _(pe):
            pe.wait_ge(wpq_in, 16)
            pe.wait_ge(dve_const, 1)

            def pre_products(s, h, gather=False):
                for c in range(h * HALF, (h + 1) * HALF):
                    own = gather and c == CH - 1
                    acc = ps_pre(s, h)[:, (c % HALF) * P:(c % HALF + 1) * P]
                    last = nc.tensor.matmul(acc, lhs[s][:, c * P:(c + 1) * P], rhs[s][:, :], start=True, stop=not own)
                    if own:
                        for t in range(HI):
                            for k in range(3):
                                last = nc.tensor.matmul(acc, shot[s][:, t, :], p_part[k][:, t, :], start=False,
                                                        stop=(t == HI - 1 and k == 2))
                return last

            def scatter_products(p, s):
                if p == 0:
                    for c in range(CH):
                        nc.tensor.matmul(ps_cw(s), tally[s][:, c, :], hot_bf(s)[:, c, :],
                                         start=(c == 0), stop=(c == CH - 1))
                for c in range(CH):
                    last = nc.tensor.matmul(ps_agg(s), (msg if p < 2 else gat)[s][:, c, :],
                                            hot[s][:, c, (0 if p < 2 else 1), :], start=(c == 0), stop=(c == CH - 1))
                return last

            for p in range(3):
                if p < 2:
                    for a, copied, done in ((0, p_copied, p_mm), (1, q_copied, q_mm)):
                        for j in range(TILES // 2):
                            if a == 0 and p:
                                pe.wait_ge(m_added, j + 1)
                                if j == 0:
                                    pe.wait_ge(cb_added, NBLK)
                            if j >= 4:
                                pe.wait_ge(copied, 13 * p + j - 3)
                            for t in (2 * j, 2 * j + 1):
                                if a == 0 and p == 0 and t % PIECES[0][1] == 0:
                                    pe.wait_ge(x_in[t // PIECES[0][1]], 16)
                                mm = nc.tensor.matmul(ps[:, 4 * a + j % 4, (t % 2) * P:(t % 2 + 1) * P],
                                                      hT[:, t * P:(t + 1) * P], wpq[:, a, :], start=True, stop=True)
                            mm.then_inc(done, 1)
                    pe.wait_ge(p_copied, 13 * (p + 1))
                    pe.wait_ge(q_copied, 13 * (p + 1))
                if p == 0:
                    pe.wait_ge(flag_ready, 1)
                    fast = pe.value_load(flag[0:1, 0:1], min_val=0, max_val=1)
                    pe.wait_ge(const_in, 16 * 5)
                    pe.wait_ge(pool_const, 10)
                    pe.wait_ge(dve_const, 8)
                    for s in range(2):
                        pe.wait_ge(rhs_const[s], 16)
                if p == 1:
                    for t in range(TILES):
                        mm = nc.tensor.matmul(ps[:, 7, t:t + 1], cw[:, t * P:(t + 1) * P], parts[:, 0:1],
                                              start=True, stop=True)
                    mm.then_inc(deg_mm, 1)
                with pe.If(fast == 1):
                    def products(g, s, k, own):
                        n = nth(p, g)
                        pe.wait_ge(oht_made, n + 1)
                        pe.wait_ge(ea_in[s], 16 * used(p, s, k))
                        pe.wait_ge(qw_in[s], 16 * used(p, s, k))
                        for h in range(2):
                            if again(p, g):
                                pe.wait_ge(pre_added, 2 * (n - 2) + h + 1)
                            if h == 1 and own:
                                pe.wait_ge(shot_made, n + 1)
                                pe.wait_ge(part_left, 2 * len(QUADS) * (p + 1))
                                pe.wait_ge(part_cut, 2 * len(QUADS) * (p + 1))
                            pre_products(s, h, gather=own).then_inc(pre_mm, 1)

                    def sums(g, s):
                        n = nth(p, g)
                        pe.wait_ge(relu_done, 2 * n + 2)
                        if p == 0:
                            pe.wait_ge(hotw_made, g + 1)
                        else:
                            pe.wait_ge(hot_made, n + 1)
                        if again(p, g):
                            pe.wait_ge(agg_added, n - 1)
                        scatter_products(p, s).then_inc(scat_mm, 1)

                    def step(g, s, k, first, whole, own, own_next):
                        if type(g) is not int or g < NG - 1:
                            products(g + 1, 1 - s, k + s, own_next)
                        sums(g, s)

                    def adjacency(q, m, first):
                        n = q * 2 + m
                        pe.wait_ge(ehot_made, 2 * n + 2)
                        pe.wait_ge(low_made, n + 1)
                        for b in range(CH // 2):
                            if not (first and m == 0):
                                pe.wait_ge(adj_copied, (n - 1) * (CH // 2) + b + 1)
                            for c in (2 * b, 2 * b + 1):
                                for w in range(3):
                                    mm = nc.tensor.matmul(ps[:, b, (c % 2) * KEYS:(c % 2 + 1) * KEYS],
                                                          low[m][:, c, w, :], khot[m][:, c, :],
                                                          start=(w == 0), stop=(w == 2))
                            mm.then_inc(adj_mm, 1)

                    def block_sums(q, slot, first):
                        pe.wait_ge(adj_copied, (q + 1) * CH)
                        if not first:
                            pe.wait_ge(part_copied, q)
                        for t in range(HI):
                            mm = nc.tensor.matmul(ps[:, 6, 0:2 * CH * CW], node_b[:, t, :], blocks[slot][:, t, :],
                                                  start=(t == 0), stop=(t == HI - 1))
                        mm.then_inc(part_mm, 1)

                    def turn_sums(q, added):
                        pe.wait_ge(part_copied, q + 1)
                        if added is not None:
                            pe.wait_ge(sums_added, added)
                        nc.tensor.transpose(ps[:, 7, 0:P], part[:, :], ident[:, :]).then_inc(partT_mm, 1)

                    def merge_sums(q, slot):
                        pe.wait_ge(partT_copied, q + 1)
                        pe.wait_ge(mrg_made, q + 1)
                        nc.tensor.matmul(ps[:, 7, 0:2 * W], partT[:, :], mrg[slot][:, :], start=True, stop=True
                                         ).then_inc(merge_mm, 1)

                    def scatter3(m, slot, i, at, added):
                        for h in range(2):
                            pe.wait_ge(rows_in[slot][h], rows_of3(slot, h, i, at))
                        pe.wait_ge(photw_made, m + 1)
                        if added is not None:
                            pe.wait_ge(sums_added, added)
                        scatter_products(2, slot).then_inc(pscat_mm, 1)

                    def step3(i, at, g, n):
                        r = TURN[:at].count(TURN[at])
                        start = type(i) is int
                        if TURN[at] == "P":
                            scatter3(n, r % 2, i, at, None if start and r < 2 else adds(i, at))
                            return
                        adjacency(n, 0, start and r == 0)
                        if not (start and r < 2):
                            turn_sums(n - 2, None if start and r == 2 else adds(i, at))
                        if not (start and r < 1):
                            block_sums(n - 1, (r + 1) % 2, start and r == 1)
                        if not (start and r < 2):
                            merge_sums(n - 2, (r + 1) % 3)
                        adjacency(n, 1, False)
                    if p < 2:
                        products(0, 0, 1, False)
                        groups(pe, step)
                    else:
                        turns(pe, step3)
                        done = TG * TURNS - 2 * E_LAG - P_LAG
                        turn_sums(E_LAST - 2, done + 2)
                        block_sums(E_LAST - 1, 1, False)
                        merge_sums(E_LAST - 2, (E_LAST - 2) % 3)
                        turn_sums(E_LAST - 1, done + 6)
                        merge_sums(E_LAST - 1, (E_LAST - 1) % 3)
                        scatter3(P_LAST, 0, TURNS - 1, None, done + 3)
                with pe.Else():
                    with pe.Fori(0, NG) as g:
                        n = nth(p, g)
                        if p < 2:
                            pe.wait_ge(g_lhs, n + 1)
                            pe.wait_ge(g_ea, 16 * (n + 1))
                            pe.wait_ge(g_qw, 16 * (n + 1))
                            for h in range(2):
                                last = pre_products(0, h)
                            last.then_inc(g_pre, 1)
                            pe.wait_ge(g_relu, n + 1)
                        else:
                            pe.wait_ge(g_rows, 16 * CH * (n + 1))
                        pe.sem_inc(passed, 1)
                        with pe.Fori(0, NWIN) as w:
                            pe.wait_ge(g_hot, n * NWIN + w + 1)
                            scatter_products(p, 0).then_inc(g_scat, 1)
                def counted(b):
                    if b >= 4:
                        pe.wait_ge(cb_added, b - 3)
                    nc.tensor.matmul(ps[:, b % 4, 0:BLK], be2_row[:, :], cw[:, b * BLK:(b + 1) * BLK],
                                     start=True, stop=True).then_inc(cb_mm, 1)

                def updated(b):
                    nc.tensor.matmul(ps[:, 4 + b % 4, 0:BLK], we2[:, :], aggT[:, b * BLK:(b + 1) * BLK],
                                     start=True, stop=True).then_inc(m_mm, 1)
                if p == 0:
                    pe.wait_ge(agg_clear, 1)
                    for b in range(NBLK):
                        counted(b)
                        if b >= 4:
                            pe.wait_ge(m_added, b - 3)
                        updated(b)
                if p == 1:
                    pe.wait_ge(agg_clear, 3)
                    pe.wait_ge(dchain, 1)
                    for b in range(NBLK + 2):
                        if b < NBLK:
                            if b >= 4:
                                pe.wait_ge(m_added, NBLK + b - 3)
                            updated(b)
                        if b >= 2:
                            q = (b - 2) // 2
                            pe.wait_ge(m_added, NBLK + b - 1)
                            if q >= 4 and b % 2 == 0:
                                pe.wait_ge(u_copied, q - 3)
                            pe.sem_inc(passed, 1)
                            for t in (2 * b - 4, 2 * b - 3):
                                tr = nc.tensor.transpose(ps[:, q % 4, t % 4 * P:(t % 4 + 1) * P],
                                                         hT[:, t * P:(t + 1) * P], ident[:, :])
                            if b % 2 or b == NBLK + 1:
                                tr.then_inc(u_tr, 1)
                    pe.wait_ge(u_copied, len(QUADS))
                    for q, (t0, n) in enumerate(QUADS):
                        pe.wait_ge(z_even, (t0 + n) // 2)
                        pe.wait_ge(z_odd, (t0 + n) // 2)
                        if q >= 4:
                            pe.wait_ge(z_copied, q - 3)
                        for t in range(t0, t0 + n):
                            tr = nc.tensor.transpose(ps[:, q % 4, (t - t0) * P:(t - t0 + 1) * P],
                                                     node_b[:, t, :], ident[:, :])
                        tr.then_inc(z_tr, 1)
                    pe.wait_ge(z_copied, len(QUADS))
            pe.wait_ge(agg_clear, 4)
            for q, (t0, n) in enumerate(QUADS):
                if q >= 4:
                    pe.wait_ge(y_scaled, QUADS[q - 4][0] + QUADS[q - 4][1])
                for t in range(t0, t0 + n):
                    mm = nc.tensor.matmul(ps[:, q % 4, (t - t0) * P:(t - t0 + 1) * P],
                                          aggT[:, t * P:(t + 1) * P], w1t[:, :], start=True, stop=True)
                mm.then_inc(y_mm, 1)

        @block.scalar
        def _(act):
            for i in range(1, len(PIECES), 2):
                cols = slice(PIECES[i][0] * P, min(sum(PIECES[i]) * P, NODES))
                act.dma_start(hT[:, cols], xT[:, cols]).then_inc(x_in[i], 16)

            def split_weight(k):
                nc.scalar.copy(w_part[k], ws[:, :] if k == 0 else w_left).then_inc(w_split, 1)
                act.wait_ge(w_split, 2 * k + 1)
                nc.scalar.copy(wp[:, k, :], w_part[k]).then_inc(w_kept, 1)

            for p in range(3):
                if p < 2:
                    if p:
                        act.wait_ge(p_out, 16 * len(QUADS))
                    for j in range(TILES // 2):
                        act.wait_ge(p_mm, 13 * p + j + 1)
                        nc.scalar.copy(node_a[:, 2 * j:2 * j + 2, :],
                                       ps[:, j % 4, 0:2 * P].rearrange("p (t f) -> p t f", t=2)
                                       ).then_inc(p_copied, 1)
                        if j % 2 or j == TILES // 2 - 1:
                            t0, n = QUADS[j // 2]
                            act.wait_ge(p_copied, 13 * p + j + 1)
                            act.dma_start(p_dram.rearrange("(t p) f -> p t f", p=P)[:, t0:t0 + n, :],
                                          node_a[:, t0:t0 + n, :]).then_inc(p_out, 16)
                    if p == 0:
                        act.wait_ge(flag_ready, 1)
                        fast = act.value_load(flag[0:1, 0:1], min_val=0, max_val=1)
                    for q, (t0, n) in enumerate(QUADS):
                        n = min(n, HI - t0)
                        nc.scalar.copy(p_part[0][:, t0:t0 + n, :], node_a[:, t0:t0 + n, :]).then_inc(part_cut, 1)
                    for q, (t0, n) in enumerate(QUADS):
                        n = min(n, HI - t0)
                        act.wait_ge(part_left, 2 * len(QUADS) * p + q + 1)
                        nc.scalar.copy(p_part[1][:, t0:t0 + n, :], rest[:, t0:t0 + n, :]).then_inc(part_cut, 1)
                    if p == 0:
                        act.wait_ge(meta_in, 48)
                        for k in range(3):
                            if k:
                                act.wait_ge(w_split, 2 * k)
                            split_weight(k)
                    else:
                        act.wait_ge(dchain, 3)
                        nc.scalar.activation(dtmp[:, :], dtmp[:, :], ACT.Sqrt).then_inc(ln_std, 1)
                    with act.If(fast == 1):
                        def relu(g, s, k, first, whole, own, own_next):
                            for h in range(2):
                                act.wait_ge(pre_added, 2 * nth(p, g) + h + 1)
                                m = msg[s][:, h * HALF:(h + 1) * HALF, :]
                                nc.scalar.activation(m, m, ACT.Relu).then_inc(relu_done, 1)
                        groups(act, relu)
                    with act.Else():
                        with act.Fori(0, NG) as g:
                            act.wait_ge(g_add, 2 * nth(p, g) + 2)
                            nc.scalar.activation(msg[0][:, :, :], msg[0][:, :, :], ACT.Relu).then_inc(g_relu, 1)
                if p == 1:
                    act.wait_ge(p_out, 2 * 16 * len(QUADS))
                    for q, (t0, n) in enumerate(QUADS):
                        act.wait_ge(u_tr, q + 1)
                        nc.scalar.copy(node_a[:, t0:t0 + n, :],
                                       ps[:, q % 4, 0:n * P].rearrange("p (t f) -> p t f", f=P)).then_inc(u_copied, 1)
                    act.wait_ge(ln_var, TILES)
                    nc.scalar.activation(std[:, :], mv[:, :, 1], ACT.Sqrt, bias=eps[:, 0:1]).then_inc(ln_std, 1)
                    act.wait_ge(q_out, 2 * 16 * len(QUADS))
                    act.wait_ge(ln_scale, 2)
                    for t in range(1, TILES, 2):
                        nc.scalar.activation(node_b[:, t, :], node_a[:, t, :], ACT.Identity, bias=zshift[:, t:t + 1],
                                             scale=zscale[:, t:t + 1]).then_inc(z_odd, 1)
                    for q, (t0, n) in enumerate(QUADS):
                        act.wait_ge(z_tr, q + 1)
                        nc.scalar.copy(aggT[:, t0 * P:(t0 + n) * P], ps[:, q % 4, 0:n * P]).then_inc(z_copied, 1)
            def twice_x():
                act.wait_ge(ln_scale, 4)
                for t in range(1, TILES, 2):
                    nc.scalar.activation(x1[:, t, :], node_a[:, t, :], ACT.Identity, bias=xshift[:, t:t + 1],
                                         scale=xscale[:, t:t + 1]).then_inc(x_odd, 1)
            with act.If(fast == 1):
                def copy_block(q, m, slot, first):
                    if not first:
                        act.wait_ge(part_mm, q - 1)
                    for b in range(CH // 2):
                        act.wait_ge(adj_mm, (q * 2 + m) * (CH // 2) + b + 1)
                        k = (m * CH + 2 * b) * CW
                        nc.scalar.copy(blocks[slot][:, :, k:k + 2 * CW].rearrange("p t (c j) -> p c t j", c=2),
                                       ps[:, b, 0:2 * KEYS].rearrange("p (c t j) -> p c t j", c=2, t=HI)
                                       ).then_inc(adj_copied, 1)

                def weigh_low(g, q, m, first):
                    if not first:
                        act.wait_ge(adj_mm, ((q - 1) * 2 + m + 1) * (CH // 2))
                    for c in range(DIRECT, CH):
                        if c in (DIRECT, HALF):
                            act.wait_ge(ehot_made, (q * 2 + m) * 2 + c // HALF + 1)
                        at = bass.ds((g + m) * CH + c, 1)
                        for w in (1, 2):
                            last = nc.scalar.mul(low[m][:, c, w, :], lowhot[m][:, c, :], wp[:, w, at])
                    last.then_inc(low_made, 1)

                def copy_sums(q, first):
                    act.wait_ge(part_mm, q + 1)
                    if not first:
                        act.wait_ge(partT_mm, q)
                    nc.scalar.copy(part[:, :], ps[:, 6, 0:2 * CH * CW]).then_inc(part_copied, 1)

                def copy_turned(q, first):
                    act.wait_ge(partT_mm, q + 1)
                    if not first:
                        act.wait_ge(merge_mm, q)
                    nc.scalar.copy(partT[:, :], ps[:, 7, 0:P]).then_inc(partT_copied, 1)

                def step3(i, at, g, n):
                    r = TURN[:at].count(TURN[at])
                    start = type(i) is int
                    if TURN[at] == "P":
                        return
                    weigh_low(g, n, 0, start and r < 1)
                    if not (start and r < 2):
                        copy_sums(n - 2, start and r == 2)
                    if not (start and r < 1):
                        copy_block(n - 1, 1, (r + 1) % 2, start and r < 3)
                    if start and r == 1:
                        act.wait_ge(x_even, TILES // 2)
                        act.wait_ge(x_odd, TILES // 2)
                    weigh_low(g, n, 1, start and r < 1)
                    copy_block(n, 0, r % 2, start and r < 2)
                    if not (start and r < 2):
                        copy_turned(n - 2, start and r == 2)
                    if start and r == 0:
                        twice_x()
                turns(act, step3)
                copy_sums(E_LAST - 2, False)
                copy_block(E_LAST - 1, 1, 1, False)
                copy_turned(E_LAST - 2, False)
                copy_sums(E_LAST - 1, False)
                copy_turned(E_LAST - 1, False)
            with act.Else():
                twice_x()
                act.wait_ge(x_even, TILES // 2)
                act.wait_ge(x_odd, TILES // 2)
            for q, (t0, n) in enumerate(QUADS):
                act.wait_ge(y_mm, q + 1)
                for t in range(t0, t0 + n):
                    nc.scalar.mul(node_a[:, t, :], ps[:, q % 4, (t - t0) * P:(t - t0 + 1) * P], dinv[:, t:t + 1]
                                  ).then_inc(y_scaled, 1)
            act.wait_ge(ln_var, 2 * TILES)
            nc.scalar.activation(std[:, :], mv[:, :, 1], ACT.Sqrt, bias=eps[:, 0:1]).then_inc(ln_std, 1)
            act.wait_ge(ln_scale, 5)
            for t in OUT_ACT:
                nc.scalar.activation(node_b[:, t, :], node_a[:, t, :], ACT.Identity, bias=xshift[:, t:t + 1],
                                     scale=rstd[:, t:t + 1]).then_inc(out_act, 1)

        @block.vector
        def _(dve):
            V = nc.vector
            V.memset(hT[:, NODES:NPAD], 0.0).then_inc(dve_const, 1)
            V.memset(be2_row[:, :], 0.0).then_inc(dve_const, 1)
            V.memset(parts[:, :], 1.0).then_inc(dve_const, 1)
            dve.wait_ge(dve_const, 3)
            V.memset(parts[0:1, :], 0.0).then_inc(dve_const, 1)
            V.memset(ones[:, :], 1.0).then_inc(dve_const, 1)
            V.memset(eps[:, :], EPS).then_inc(dve_const, 1)
            for s in range(2):
                V.memset(tally[s][:, :, :], 1.0).then_inc(dve_const, 1)
            for s in range(3):
                V.memset(mrg[s][:, :], 0.0).then_inc(mrg_clear, 1)
            dve.wait_ge(grp_in, 16)
            V.tensor_reduce(cmin[:, :], dgrp, AX.X, ALU.min).then_inc(bounds, 1)
            V.scalar_tensor_tensor(dreal, dgrp, float(NODES), dgrp, ALU.is_lt, ALU.mult
                                   ).then_inc(bounds, 1)
            dve.wait_ge(bounds, 2)
            V.tensor_reduce(cmax[:, :], dreal, AX.X, ALU.max).then_inc(bounds, 1)
            V.tensor_reduce(bmin[:, :], cmin[:, :], AX.X, ALU.min).then_inc(bounds, 1)
            V.tensor_copy(cint[:, :], cmin[:, :]).then_inc(bounds, 1)
            dve.wait_ge(bounds, 5)
            V.tensor_reduce(bmax[:, :], cmax[:, :], AX.X, ALU.max).then_inc(bounds, 1)
            V.tensor_tensor(cspan[:, :], cmax[:, :], cmin[:, :], ALU.subtract).then_inc(bounds, 1)
            V.tensor_copy(bint[:, :], bmin[:, :]).then_inc(bounds, 1)
            dve.wait_ge(bounds, 8)
            V.tensor_tensor(spans[:, 0:1], bmax[:, :], bmin[:, :], ALU.subtract).then_inc(bounds, 1)
            V.tensor_reduce(spans[:, 1:2], cspan[:, :], AX.X, ALU.max).then_inc(bounds, 1)

            def flags():
                dve.wait_ge(base_in, 64)
                V.tensor_reduce(span_max[:, :], span_row[:, :].rearrange("a (n k) -> a k n", k=2), AX.X, ALU.max
                                ).then_inc(bounds, 1)
                dve.wait_ge(bounds, 11)
                V.tensor_single_scalar(fits[:, 0:1], span_max[:, 0:1], float(W), ALU.is_lt).then_inc(bounds, 1)
                V.tensor_single_scalar(fits[:, 1:2], span_max[:, 1:2], float(CW), ALU.is_lt).then_inc(bounds, 1)
                dve.wait_ge(bounds, 13)
                V.tensor_tensor(flag[:, :], fits[:, 0:1], fits[:, 1:2], ALU.mult).then_inc(flag_ready, 1)

            def chunk_keys():
                V.tensor_single_scalar(src_hi, srcs, 7, ALU.arith_shift_right).then_inc(chunk_ready, 1)
                V.tensor_single_scalar(srcs, srcs, P - 1, ALU.bitwise_and).then_inc(chunk_ready, 1)
                V.tensor_tensor(key[:, :], dsts[:, :], cbase, ALU.subtract).then_inc(chunk_ready, 1)
                V.tensor_scalar(lane_hi[:, :], lane[:, :], CH * CW - 1, CW.bit_length() - 1, ALU.bitwise_and,
                                ALU.arith_shift_right).then_inc(chunk_ready, 1)
                V.tensor_single_scalar(lane_lo[:, :], lane[:, :], CW - 1, ALU.bitwise_and).then_inc(chunk_ready, 1)
                dve.wait_ge(chunk_ready, 5)
                V.tensor_copy(lo[:, :], srcs).then_inc(chunk_ready, 1)
                V.scalar_tensor_tensor(key[:, :], src_hi, float(CW), key[:, :], ALU.mult, ALU.add
                                       ).then_inc(chunk_ready, 1)
                V.tensor_copy(lane_hif[:, :], lane_hi[:, :]).then_inc(chunk_ready, 1)
                V.tensor_copy(lane_lof[:, :], lane_lo[:, :]).then_inc(chunk_ready, 1)
                dve.wait_ge(chunk_ready, 9)
                V.tensor_scalar(mine[:, :], iota_row[:, 0:CH], lane_hif[:, 0:1], None, ALU.is_equal
                                ).then_inc(chunk_ready, 1)
                dve.wait_ge(chunk_ready, 10)
                V.tensor_tensor(picked.rearrange("r (g c) -> r g c", c=CH), cbase.rearrange("r (g c) -> r g c", c=CH),
                                mine[:, :].unsqueeze(1).to_broadcast([P, NG, CH]), ALU.mult).then_inc(chunk_ready, 1)
                dve.wait_ge(chunk_ready, 11)
                V.tensor_reduce(mcol[:, :], picked.rearrange("r (g c) -> r g c", c=CH), AX.X, ALU.add
                                ).then_inc(chunk_ready, 1)
                dve.wait_ge(chunk_ready, 12)
                V.scalar_tensor_tensor(mcol[:, :], mcol[:, :], lane_lof[:, 0:1], base_bc[:, :], ALU.add, ALU.subtract
                                       ).then_inc(chunk_ready, 1)
                V.memset(xTs[:, NODES:NPAD], 0.0).then_inc(chunk_ready, 1)

            def one_hot(s, ids, window):
                return V.tensor_tensor(hot[s][:, :, 0, :], window[:, :].unsqueeze(1).to_broadcast([P, CH, W]),
                                       ids.unsqueeze(2).to_broadcast([P, CH, W]), ALU.is_equal)

            def tally_up(s, g):
                V.tensor_copy(tally[s][:, :, 1:4].rearrange("p c w -> p w c"), wp[:, :, bass.ds(g * CH, CH)])
                return V.tensor_copy(hot_bf(s), hot[s][:, :, 0, :])

            def weigh(s, g):
                return V.tensor_tensor(hot[s][:, :, 1, :], hot[s][:, :, 0, :],
                                       ws[:, bass.ds(g * CH, CH)].unsqueeze(2).to_broadcast([P, CH, W]), ALU.mult)

            def join():
                dve.wait_ge(m_added, NBLK)
                dve.wait_ge(cb_added, NBLK)
                V.scalar_tensor_tensor(xTs[:, :], hT[:, :], bias0_col[:, 0:1], xTs[:, :], ALU.add, ALU.add
                                       ).then_inc(x_joined, 1)
                dve.wait_ge(ln_std, 1)
                V.reciprocal(dtmp[:, :], dtmp[:, :]).then_inc(dchain, 1)
                dve.wait_ge(dchain, 4)
                V.tensor_tensor(dinv[:, :], dtmp[:, :], dmask[:, :], ALU.mult).then_inc(dchain, 1)

            def fast_steps(eng, one_hots, scatter_hots, vector_step, add_window, p):
                one_hots(0, 0, 1, False)
                scatter_hots(0, 0)
                groups(eng, vector_step)
                eng.wait_ge(agg_added, nth(p, NG - 1))
                add_window(NG - 1, 0)
                eng.wait_ge(agg_added, nth(p, NG))

            def weight_left(k):
                dve.wait_ge(w_split, 2 * k + 1)
                V.tensor_tensor(w_left, ws[:, :] if k == 0 else w_left, w_part[k], ALU.subtract).then_inc(w_split, 1)

            def twice_x():
                dve.wait_ge(ln_scale, 4)
                for t in range(0, TILES, 2):
                    V.tensor_scalar(x1[:, t, :], node_a[:, t, :], mv[:, t, 0:1], xscale[:, t:t + 1],
                                    ALU.subtract, ALU.mult).then_inc(x_even, 1)

            dve.wait_ge(be1_in, 16)
            for p in range(3):
                if p < 2:
                    if p == 0:
                        flags()
                    if p:
                        dve.wait_ge(q_out, 16 * len(QUADS))
                    for j in range(TILES // 2):
                        dve.wait_ge(q_mm, 13 * p + j + 1)
                        V.tensor_tensor(node_b[:, 2 * j:2 * j + 2, :],
                                        ps[:, 4 + j % 4, 0:2 * P].rearrange("p (t f) -> p t f", t=2),
                                        be1_bc[:, :].unsqueeze(1).to_broadcast([P, 2, P]), ALU.add
                                        ).then_inc(q_copied, 1)
                    if p == 0:
                        dve.wait_ge(flag_ready, 1)
                        fast = dve.value_load(flag[0:1, 0:1], min_val=0, max_val=1)
                        dve.wait_ge(pool_const, 10)
                        V.tensor_scalar(base_p[:, :], base_bc[:, :], iota_col[:, 0:1], None, ALU.add
                                        ).then_inc(rel_ready, 1)
                        dve.wait_ge(meta_in, 48)
                        V.tensor_tensor(drel[:, :].rearrange("p (g c) -> p g c", c=CH),
                                        dsts[:, :].rearrange("p (g c) -> p g c", c=CH),
                                        base_bc[:, :].unsqueeze(2).to_broadcast([P, NG, CH]), ALU.subtract
                                        ).then_inc(rel_ready, 1)
                    base = 2 * len(QUADS) * p

                    def left_of(q):
                        t0, n = QUADS[q]
                        n = min(n, HI - t0)
                        dve.wait_ge(part_cut, base + q + 1)
                        V.tensor_tensor(rest[:, t0:t0 + n, :], node_a[:, t0:t0 + n, :], p_part[0][:, t0:t0 + n, :],
                                        ALU.subtract).then_inc(part_left, 1)
                    dve.wait_ge(q_out, 16 * len(QUADS) * (p + 1))
                    for q in range(len(QUADS)):
                        left_of(q)
                    for q, (t0, n) in enumerate(QUADS):
                        n = min(n, HI - t0)
                        dve.wait_ge(part_cut, base + len(QUADS) + q + 1)
                        V.tensor_tensor(p_part[2][:, t0:t0 + n, :], rest[:, t0:t0 + n, :], p_part[1][:, t0:t0 + n, :],
                                        ALU.subtract).then_inc(part_left, 1)
                    dve.wait_ge(part_left, base + 2 * len(QUADS))
                    dve.wait_ge(p_out, 16 * len(QUADS) * (p + 1))
                    if p == 0:
                        weight_left(0)
                        weight_left(1)
                        dve.wait_ge(w_kept, 3)
                        dve.wait_ge(rel_ready, 2)
                        dve.wait_ge(dve_const, 8)
                        dve.wait_ge(const_in, 16 * 5)
                    else:
                        dve.wait_ge(deg_mm, 1)
                        V.tensor_scalar_add(deg[:, :], ps[:, 7, 0:TILES], 1.0).then_inc(dchain, 1)
                        dve.wait_ge(dchain, 1)
                        V.tensor_single_scalar(dmask[:, :], deg[:, :], 0.0, ALU.is_gt).then_inc(dchain, 1)
                        dve.wait_ge(dchain, 2)
                        V.tensor_copy(dtmp[:, :], ones[:, 0:1].to_broadcast([P, TILES])).then_inc(bounds, 1)
                        dve.wait_ge(bounds, 14)
                        V.copy_predicated(dtmp[:, :], dmask[:, :].bitcast(mybir.dt.uint32), deg[:, :]
                                          ).then_inc(dchain, 1)
                        dve.wait_ge(agg_clear, 2)
                with dve.If(fast == 1):
                    def add_window(g, s):
                        n = nth(p, g)
                        dve.sem_inc(passed, 1)
                        b = dve.value_load(base_row[0:1, bass.ds(g, 1)], min_val=0, max_val=NODES - 1)
                        dve.wait_ge(scat_mm, n + 1)
                        if p == 0:
                            c = cw[:, bass.ds(b, W)]
                            V.tensor_tensor(c, c, ps_cw(s), ALU.add)
                        a = aggT[:, bass.ds(b, W)]
                        V.tensor_tensor(a, a, ps_agg(s), ALU.add).then_inc(agg_added, 1)

                    def one_hots(g, s, k, own):
                        n = nth(p, g)
                        dve.wait_ge(dbc_in[s], 16 * used(p, s, k))
                        if again(p, g):
                            dve.wait_ge(pre_mm, 2 * (n - 1))
                        V.tensor_scalar(lhs[s][0:W, :], dbc[s][:, :], base_p[0:W, bass.ds(g, 1)], None,
                                        ALU.is_equal).then_inc(oht_made, 1)
                        dve.wait_ge(sbc_in[s], 16 * used(p, s, k))
                        if p > 0 or type(g) is not int or g > 0:
                            dve.wait_ge(shot_made, n)
                        V.tensor_scalar(sbc16[:, :], sbc[s][:, :], float(MID), None, ALU.subtract).then_inc(sbc_cut, 1)
                        dve.wait_ge(sbc_cut, n + 1)
                        if not own:
                            V.memset(scratch[:, :], 0.0).then_inc(shot_made, 1)
                        else:
                            V.tensor_tensor(shot[s], numbers, sbc16[:, :].unsqueeze(1).to_broadcast([P, HI, P]),
                                            ALU.is_equal).then_inc(shot_made, 1)

                    def scatter_hots(g, s):
                        n = nth(p, g)
                        if again(p, g):
                            dve.wait_ge(scat_mm, n - 1)
                        one_hot(s, drel[:, bass.ds(g * CH, CH)], iota_row).then_inc(hot_made, 1)
                        if p == 0:
                            dve.wait_ge(hot_made, n + 1)
                            tally_up(s, g).then_inc(hotw_made, 1)

                    def vector_step(g, s, k, first, whole, own, own_next):
                        n = nth(p, g)
                        more = type(g) is not int or g < NG - 1
                        if more:
                            one_hots(g + 1, 1 - s, k + s, own_next)
                        if again(p, g):
                            dve.wait_ge(scat_mm, n - 1)
                        for h in range(2):
                            dve.wait_ge(rows_in[s][h], rows_of(s, h, used(p, s, k), p * WHOLE[s] + whole))
                            dve.wait_ge(pre_mm, 2 * n + h + 1)
                            V.tensor_tensor(msg[s][:, h * HALF:(h + 1) * HALF, :],
                                            ps_pre(s, h).rearrange("p (c f) -> p c f", f=P),
                                            gat[s][:, h * HALF:(h + 1) * HALF, :], ALU.add).then_inc(pre_added, 1)
                        if not own and more:
                            dve.wait_ge(pre_added, 2 * n + 2)
                            V.memset(gat[s][:, CH - 1, :], 0.0)
                        if type(g) is not int or g > 0:
                            if again(p, g):
                                dve.wait_ge(agg_added, n - 1)
                            add_window(g - 1, 1 - s)
                        if more:
                            scatter_hots(g + 1, 1 - s)
                        if type(g) is int and g == 1:
                            (chunk_keys if p == 0 else join)()

                    def add_sums(kind, g, n, bank, before):
                        if before is None:
                            dve.wait_ge(z_copied, len(QUADS))
                        for m in range(SIZE[kind]):
                            dve.sem_inc(passed, 1)
                            b = dve.value_load(base_row[0:1, bass.ds(g + m, 1)], min_val=0, max_val=NODES - 1)
                            dve.wait_ge(merge_mm if kind == "E" else pscat_mm, n + 1)
                            if before is not None or m > 0:
                                dve.wait_ge(sums_added, m if before is None else before + m)
                            a = aggT[:, bass.ds(b, W)]
                            V.tensor_tensor(a, a, ps[:, bank, m * W:(m + 1) * W], ALU.add).then_inc(sums_added, 1)

                    def e_hots(g, q, m, first):
                        if not first:
                            dve.wait_ge(adj_mm, ((q - 1) * 2 + m + 1) * (CH // 2))
                        for c in range(CH):
                            at = bass.ds((g + m) * CH + c, 1)
                            V.tensor_scalar(khot[m][:, c, :], iota_key[:, :], key[:, at], None, ALU.is_equal)
                            for w in range(3 if c < DIRECT else 1):
                                last = V.tensor_scalar(low[m][:, c, w, :], iota_lo[:, :], lo[:, at], wp[:, w, at],
                                                       ALU.is_equal, ALU.mult)
                            if c >= DIRECT:
                                last = V.tensor_scalar(lowhot[m][:, c, :], iota_lo[:, :], lo[:, at], None,
                                                       ALU.is_equal)
                            if c % HALF == HALF - 1:
                                last.then_inc(ehot_made, 1)

                    def e_windows(g, q, slot, first):
                        if not first:
                            dve.wait_ge(merge_mm, q - 2)
                        else:
                            dve.wait_ge(mrg_clear, 3)
                        for m in range(2):
                            rows = slice(m * CH * CW, (m + 1) * CH * CW)
                            last = V.tensor_scalar(mrg[slot][rows, m * W:(m + 1) * W], iota_row[rows, :],
                                                   mcol[rows, bass.ds(g + m, 1)], None, ALU.is_equal)
                        last.then_inc(mrg_made, 1)

                    def p_hots(g, m, slot, first):
                        if not first:
                            dve.wait_ge(pscat_mm, m - 1)
                        one_hot(slot, drel[:, bass.ds(g * CH, CH)], iota_row).then_inc(phot_made, 1)
                        dve.wait_ge(phot_made, m + 1)
                        weigh(slot, g).then_inc(photw_made, 1)

                    def back(kind, r, at):
                        r -= E_LAG if kind == "E" else P_LAG
                        per = E_TURN if kind == "E" else P_TURN
                        here = groups_in(TURN[:at])
                        return here - groups_in(TURN[:place(kind, r % per)]) + (0 if r >= 0 else TG)

                    def step3(i, at, g, n):
                        r = TURN[:at].count(TURN[at])
                        start = type(i) is int
                        count = adds(i, at) - SIZE[TURN[at]]
                        if start and count < 1:
                            count = None
                        if TURN[at] == "P":
                            p_hots(g, n, r % 2, start and r < 2)
                            if not early(i, at):
                                add_sums("P", g - back("P", r, at), n - P_LAG, 4 + r % 2, count)
                        else:
                            e_hots(g, n, 0, start and r < 1)
                            if not early(i, at):
                                add_sums("E", g - back("E", r, at), n - E_LAG, 7, count)
                            e_windows(g, n, r % 3, start and r < 3)
                            e_hots(g, n, 1, start and r < 1)
                            if start and r == 0:
                                twice_x()

                    if p == 2:
                        turns(dve, step3)
                        p_hots(NG - 1, P_LAST, 0, False)
                        done = TG * TURNS - 2 * E_LAG - P_LAG
                        for kind, n in (("E", E_LAST - 3), ("P", P_LAST - 2), ("P", P_LAST - 1), ("E", E_LAST - 2),
                                        ("E", E_LAST - 1), ("P", P_LAST)):
                            per = E_TURN if kind == "E" else P_TURN
                            g = (NG - 1 if (kind, n) == ("P", P_LAST) else
                                 n // per * TG + groups_in(TURN[:place(kind, n % per)]))
                            add_sums(kind, g, n, 7 if kind == "E" else 4 + n % 2, done)
                            done += SIZE[kind]
                        dve.wait_ge(sums_added, done)
                    if p < 2:
                        fast_steps(dve, one_hots, scatter_hots, vector_step, add_window, p)
                    V.memset(scratch[:, :], 0.0).then_inc(agg_clear, 1)
                with dve.Else():
                    if p == 2:
                        dve.wait_ge(z_copied, len(QUADS))
                        twice_x()
                    if p == 1:
                        join()
                    if p == 0:
                        chunk_keys()
                        V.memset(lhs[0][0:W, :], 0.0).then_inc(g_group, 1)
                    with dve.Fori(0, NG) as g:
                        n = nth(p, g)
                        dve.wait_ge(g_group, n + 1)
                        if p < 2:
                            V.tensor_single_scalar(idxd[:, :], dsts[:, bass.ds(g * CH, CH)], float(NPAD - 1),
                                                   ALU.min).then_inc(g_idxd, 1)
                            V.memset(iota_win[:, :], 0.0).then_inc(g_lhs, 1)
                            dve.wait_ge(g_rows, 16 * CH * (n + 1))
                            dve.wait_ge(g_pre, n + 1)
                            V.tensor_tensor(msg[0][:, :, :], ps[:, 0:2, :].rearrange("p h (c f) -> p (h c) f", f=P),
                                            gat[0][:, :, :], ALU.add).then_inc(g_add, 1)
                            dve.wait_ge(g_rowsq, 16 * CH * (n + 1))
                            dve.wait_ge(g_add, 2 * n + 1)
                            V.tensor_tensor(msg[0][:, :, :], msg[0][:, :, :], gatq[:, :, :], ALU.add
                                            ).then_inc(g_add, 1)
                            dve.wait_ge(g_add, 2 * n + 2)
                        V.tensor_copy(iota_win[:, :], iota_row[:, :]).then_inc(g_win, 1)
                        with dve.Fori(0, NWIN) as w:
                            m = n * NWIN + w
                            dve.wait_ge(g_win, n * (NWIN + 1) + w + 1)
                            one_hot(0, dsts[:, bass.ds(g * CH, CH)], iota_win).then_inc(hot_made, 1)
                            dve.wait_ge(hot_made, m + 1)
                            (tally_up if p == 0 else weigh)(0, g).then_inc(g_hot, 1)
                            V.tensor_scalar_add(iota_win[:, :], iota_win[:, :], float(W)).then_inc(g_win, 1)
                            dve.wait_ge(g_scat, m + 1)
                            if p == 0:
                                V.tensor_tensor(cw[:, bass.ds(w * W, W)], cw[:, bass.ds(w * W, W)],
                                                ps_cw(0), ALU.add)
                            V.tensor_tensor(aggT[:, bass.ds(w * W, W)], aggT[:, bass.ds(w * W, W)], ps_agg(0),
                                            ALU.add).then_inc(g_agg, 1)
                            dve.wait_ge(g_agg, m + 1)
                        V.memset(scratch[:, :], 0.0).then_inc(g_group, 1)
                    dve.wait_ge(g_group, nth(p, NG) + 1)
                    V.memset(scratch[:, :], 0.0).then_inc(agg_clear, 1)
                if p == 0:
                    dve.wait_ge(xs_in, 16)
                    dve.wait_ge(chunk_ready, 14)

                    for b in range(NBLK):
                        cols = slice(b * BLK, (b + 1) * BLK)
                        dve.wait_ge(cb_mm, b + 1)
                        V.tensor_tensor(xTs[:, cols], ps[:, b % 4, 0:BLK], xTs[:, cols], ALU.add).then_inc(cb_added, 1)
                        dve.wait_ge(m_mm, b + 1)
                        dve.wait_ge(cb_added, b + 1)
                        V.tensor_tensor(hT[:, cols], ps[:, 4 + b % 4, 0:BLK], xTs[:, cols], ALU.add
                                        ).then_inc(m_added, 1)
                if p == 1:
                    dve.wait_ge(x_joined, 1)

                    def tile_stats(t):
                        dve.wait_ge(u_copied, t // 4 + 1)
                        V.bn_stats(stats[:, t, :], node_a[:, t, :]).then_inc(ln_stats, 1)
                    for b in range(NBLK):
                        cols = slice(b * BLK, (b + 1) * BLK)
                        dve.wait_ge(m_mm, NBLK + b + 1)
                        V.tensor_tensor(hT[:, cols], ps[:, 4 + b % 4, 0:BLK], xTs[:, cols], ALU.add
                                        ).then_inc(m_added, 1)
                        if b >= 6:
                            tile_stats(2 * b - 12)
                            tile_stats(2 * b - 11)
                    for t in range(2 * NBLK - 12, TILES):
                        tile_stats(t)
                    for t in range(TILES):
                        dve.wait_ge(ln_stats, t + 1)
                        V.bn_aggr(mv[:, t, :], stats[:, t, :]).then_inc(ln_var, 1)
                    dve.wait_ge(ln_std, 2)
                    V.reciprocal(rstd[:, :], std[:, :]).then_inc(ln_rstd, 1)
                    dve.wait_ge(ln_rstd, 1)
                    dve.wait_ge(dchain, 5)
                    dve.wait_ge(ln_var, TILES)
                    V.tensor_tensor(zscale[:, :], rstd[:, :], dinv[:, :], ALU.mult).then_inc(ln_scale, 1)
                    dve.wait_ge(ln_scale, 1)
                    V.scalar_tensor_tensor(zshift[:, :], mv[:, :, 0], -1.0, zscale[:, :], ALU.mult, ALU.mult
                                           ).then_inc(ln_scale, 1)
                    dve.wait_ge(q_out, 2 * 16 * len(QUADS))
                    for t in range(0, TILES, 2):
                        V.tensor_scalar(node_b[:, t, :], node_a[:, t, :], mv[:, t, 0:1], zscale[:, t:t + 1],
                                        ALU.subtract, ALU.mult).then_inc(z_even, 1)
                        if t == 0:
                            V.tensor_single_scalar(xscale[:, :], rstd[:, :], 2.0, ALU.mult).then_inc(ln_scale, 1)
                            dve.wait_ge(ln_scale, 3)
                            V.scalar_tensor_tensor(xshift[:, :], mv[:, :, 0], -1.0, xscale[:, :], ALU.mult, ALU.mult
                                                   ).then_inc(ln_scale, 1)
            dve.wait_ge(x_even, TILES // 2)
            dve.wait_ge(x_odd, TILES // 2)
            for q, (t0, n) in enumerate(QUADS):
                y = node_a[:, t0:t0 + n, :]
                dve.wait_ge(y_scaled, t0 + n)
                V.tensor_tensor(y, y, bias1_bc[:, :].unsqueeze(1).to_broadcast([P, n, P]), ALU.add).then_inc(y_made, 1)
                dve.wait_ge(y_made, 2 * q + 1)
                V.scalar_tensor_tensor(y, y, 0.0, x1[:, t0:t0 + n, :], ALU.max, ALU.add).then_inc(y_made, 1)
                dve.wait_ge(y_made, 2 * q + 2)
                for t in range(t0, t0 + n):
                    V.bn_stats(stats[:, t, :], node_a[:, t, :]).then_inc(ln_stats, 1)
            dve.wait_ge(z_out, 16 * len(QUADS))
            for t in range(TILES):
                dve.wait_ge(ln_stats, TILES + t + 1)
                V.bn_aggr(mv[:, t, :], stats[:, t, :]).then_inc(ln_var, 1)
            dve.wait_ge(ln_std, 3)
            V.reciprocal(rstd[:, :], std[:, :]).then_inc(ln_rstd, 1)
            dve.wait_ge(ln_rstd, 2)
            V.scalar_tensor_tensor(xshift[:, :], mv[:, :, 0], -1.0, rstd[:, :], ALU.mult, ALU.mult
                                   ).then_inc(ln_scale, 1)
            for t in OUT_DVE:
                V.tensor_scalar(node_b[:, t, :], node_a[:, t, :], mv[:, t, 0:1], rstd[:, t:t + 1],
                                ALU.subtract, ALU.mult).then_inc(out_dve, 1)


def kernel(**inputs):
    import numpy as np
    import concourse.bacc as bacc
    from concourse.bass_utils import run_bass_kernel_spmd

    f32, i32 = mybir.dt.float32, mybir.dt.int32
    pad = NG * GE - EDGES
    src = np.concatenate([np.asarray(inputs["src"]), np.zeros(pad, np.int32)])
    dst = np.concatenate([np.asarray(inputs["dst"]), np.full(pad, OFF, np.int32)])
    ew = np.concatenate([np.asarray(inputs["edge_weight"]), np.zeros(pad, np.float32)])
    ea = np.concatenate([np.asarray(inputs["edge_attr_32"]), np.zeros((pad, CE), np.float32)])
    by_lane = lambda a: np.ascontiguousarray(a.reshape(NG * CH, P).T)
    arrays = {
        "xT": np.ascontiguousarray(np.asarray(inputs["x"]).T),
        "src_g": np.ascontiguousarray(src.reshape(NG, CH, P).transpose(0, 2, 1)),
        "src_em": by_lane(src), "src_row": src, "dst_row": dst, "dst_em": by_lane(dst), "w_em": by_lane(ew),
        "eaT": np.ascontiguousarray(ea.T),
        "We1": np.asarray(inputs["L0_gnn_We1"]), "be1": np.asarray(inputs["L0_gnn_be1"]),
        "We2": np.asarray(inputs["L0_gnn_We2"]), "be2": np.asarray(inputs["L0_gnn_be2"]),
        "bias0": np.asarray(inputs["L0_gnn_bias"]),
        "W1T": np.ascontiguousarray(np.asarray(inputs["L1_gnn_weight"]).T),
        "bias1": np.asarray(inputs["L1_gnn_bias"]),
    }
    nc = bacc.Bacc("TRN2", target_bir_lowering=False, num_devices=1)
    args = {n: nc.dram_tensor(n, a.shape, mybir.dt.from_np(a.dtype), kind="ExternalInput").ap()
            for n, a in arrays.items()}
    out = nc.dram_tensor("out", (NODES, P), f32, kind="ExternalOutput").ap()
    scratch = {n: nc.dram_tensor(n, (NPAD, P), f32, kind="Internal").ap() for n in ("p_dram", "q_dram", "z_dram")}
    build(nc, out=out, base_dram=nc.dram_tensor("base_dram", (NG,), i32, kind="Internal").ap(),
          cbase_dram=nc.dram_tensor("cbase_dram", (NG * CH,), i32, kind="Internal").ap(),
          span_dram=nc.dram_tensor("span_dram", (2 * NG,), f32, kind="Internal").ap(), **scratch, **args)
    r = run_bass_kernel_spmd(nc, [arrays], core_ids=[0])
    return r.results[0]["out"]
```
